# Optimizing a Trainium2 kernel written in Bass

```python
import numpy as np
import jax
import jax.numpy as jnp

def _softmax(x, axis=-1):
    return jax.nn.softmax(x, axis=axis)

def _gelu(x):
    return jax.nn.gelu(x, approximate=True)

def _silu(x):
    return jax.nn.silu(x)

def _sigmoid(x):
    return jax.nn.sigmoid(x)

def _layernorm(x, axis=-1, eps=1e-05):
    m = jnp.mean(x, axis=axis, keepdims=True)
    v = jnp.var(x, axis=axis, keepdims=True)
    return (x - m) / jnp.sqrt(v + eps)

def _scatter_add(tgt, idx, src, axis=0):
    return tgt.at[idx].add(src)

def _segment_sum(src, seg, n):
    return jax.ops.segment_sum(src, seg, n)
kernel_name = 'mk_gnn_resnorm_d4_gnn_r32_0eb7ad'

def setup_inputs(seed: int=0):
    np.random.seed(seed)
    _w = jnp.asarray

    def _rec_inputs():
        import jax
        import jax.numpy as jnp
        _gk = jax.random.key(seed)
        x = -8.776e-05 + 1 * jax.random.normal(jax.random.fold_in(_gk, 1), (10000, 512), jnp.float32)
        src = jax.random.randint(jax.random.fold_in(_gk, 2), (5000,), 0, 10000, jnp.int32)
        dst = jax.random.randint(jax.random.fold_in(_gk, 3), (5000,), 0, 10000, jnp.int32)
        _o = jnp.argsort(dst, stable=True)
        src = src[_o]
        dst = dst[_o]
        edge_type_8 = jax.random.randint(jax.random.fold_in(_gk, 14), (5000,), 0, 8, jnp.int32)
        edge_weight = jax.random.uniform(jax.random.fold_in(_gk, 15), (5000,), jnp.float32, 0.0, 0.999999)
        return (x, src, dst, edge_type_8, edge_weight)
    x, src, dst, edge_type_8, edge_weight = _rec_inputs()

    def _L0_gnn_setup():
        import jax, jax.numpy as jnp
        import numpy as np
        LN_EPS = 1e-05
        key = jax.random.key(seed)
        k1, k2, k3, k4 = jax.random.split(key, 4)
        N, D, E = (10000, 512, 150000)
        scale = 1.0 / np.sqrt(D)
        return {'node_feature': jax.random.normal(k1, (N, D), dtype=jnp.float32), 'edge_index': jax.random.randint(k2, (2, E), 0, N, dtype=jnp.int64), 'ln_gamma': jnp.ones((D,), dtype=jnp.float32), 'ln_beta': jnp.zeros((D,), dtype=jnp.float32), 'w_l': jax.random.normal(k3, (D, D), dtype=jnp.float32) * scale, 'b_l': jnp.zeros((D,), dtype=jnp.float32), 'w_r': jax.random.normal(k4, (D, D), dtype=jnp.float32) * scale}
    _L0_gnn_all = _L0_gnn_setup()
    _L0_gnn_in = {k: v for k, v in _L0_gnn_all.items() if k in ('ln_gamma', 'ln_beta', 'w_l', 'b_l', 'w_r')}
    del _L0_gnn_all

    def _L1_gnn_setup():
        import jax, jax.numpy as jnp
        import numpy as np
        N, E, DM, H, DFF = (625, 20000, 512, 8, 64)
        DK = DM // H

        def _layernorm(x, g, b, eps=1e-05):
            mu = jnp.mean(x, axis=-1, keepdims=True)
            var = jnp.mean(jnp.square(x - mu), axis=-1, keepdims=True)
            return (x - mu) * jax.lax.rsqrt(var + eps) * g + b
        key = jax.random.key(seed)
        ks = jax.random.split(key, 12)
        s = 0.02
        h = jax.random.normal(ks[0], (N, DM), dtype=jnp.float32)
        src = jax.random.randint(ks[1], (E,), 0, N, dtype=jnp.int32)
        dst = jnp.sort(jax.random.randint(ks[2], (E,), 0, N, dtype=jnp.int32))
        return {'h': h, 'src': src, 'dst': dst, 'Wq': jax.random.normal(ks[3], (DM, DM), dtype=jnp.float32) * s, 'Wk': jax.random.normal(ks[4], (DM, DM), dtype=jnp.float32) * s, 'Wv': jax.random.normal(ks[5], (DM, DM), dtype=jnp.float32) * s, 'Wo': jax.random.normal(ks[6], (DM, DM), dtype=jnp.float32) * s, 'ln1_g': jnp.ones((DM,), jnp.float32), 'ln1_b': jnp.zeros((DM,), jnp.float32), 'ln2_g': jnp.ones((DM,), jnp.float32), 'ln2_b': jnp.zeros((DM,), jnp.float32), 'W1': jax.random.normal(ks[7], (DM, DFF), dtype=jnp.float32) * s, 'b1': jnp.zeros((DFF,), jnp.float32), 'W2': jax.random.normal(ks[8], (DFF, DM), dtype=jnp.float32) * s, 'b2': jnp.zeros((DM,), jnp.float32)}
    _L1_gnn_all = _L1_gnn_setup()
    _L1_gnn_in = {k: v for k, v in _L1_gnn_all.items() if k in ('Wq', 'Wk', 'Wv', 'Wo', 'ln1_g', 'ln1_b', 'ln2_g', 'ln2_b', 'W1', 'b1', 'W2', 'b2')}
    del _L1_gnn_all

    def _L2_gnn_setup():
        import jax, jax.numpy as jnp
        import numpy as np
        N, IN_DIM, H, D, E = (50000, 512, 8, 64, 25000)
        NEG_SLOPE = 0.2
        LN_EPS = 1e-05
        key = jax.random.key(seed)
        ks = jax.random.split(key, 8)
        x = jax.random.normal(ks[0], (N, IN_DIM), dtype=jnp.float32)
        edge_index = jax.random.randint(ks[1], (2, E), 0, N, dtype=jnp.int64)
        edge_type = jax.random.randint(ks[2], (E,), 0, 8, dtype=jnp.int64)
        edge_weight = jax.random.uniform(ks[3], (E,), dtype=jnp.float32)
        W = jax.random.normal(ks[4], (H * D, IN_DIM), dtype=jnp.float32) * (1.0 / np.sqrt(IN_DIM))
        a_src = jax.random.normal(ks[5], (H, D), dtype=jnp.float32) * (1.0 / np.sqrt(D))
        a_dst = jax.random.normal(ks[6], (H, D), dtype=jnp.float32) * (1.0 / np.sqrt(D))
        et_emb = jax.random.normal(ks[7], (8, H), dtype=jnp.float32)
        ln_gamma = jnp.ones((H * D,), dtype=jnp.float32)
        ln_beta = jnp.zeros((H * D,), dtype=jnp.float32)
        return {'x': x, 'edge_index': edge_index, 'edge_type': edge_type, 'edge_weight': edge_weight, 'W': W, 'a_src': a_src, 'a_dst': a_dst, 'et_emb': et_emb, 'ln_gamma': ln_gamma, 'ln_beta': ln_beta}
    _L2_gnn_all = _L2_gnn_setup()
    _L2_gnn_in = {k: v for k, v in _L2_gnn_all.items() if k in ('W', 'a_src', 'a_dst', 'et_emb', 'ln_gamma', 'ln_beta')}
    del _L2_gnn_all

    def _L3_gnn_setup():
        import jax, jax.numpy as jnp
        import numpy as np
        N = 625
        E = 250000
        B = 128
        Fin = 512
        Fqk = 512
        Fv = 512
        H = 8
        key = jax.random.key(seed)
        k1, k2, k3, k4 = jax.random.split(key, 4)
        x = jax.random.normal(k1, (N, Fin), dtype=jnp.float32)
        batch = jnp.sort(jax.random.randint(k2, (N,), 0, B)).astype(jnp.int32)
        ei = jax.random.randint(k3, (2, E), 0, N).astype(jnp.int32)
        W = jax.random.normal(k4, (Fin, 2 * Fqk + Fv), dtype=jnp.float32) / np.sqrt(Fin).astype(np.float32)
        return {'x': x, 'batch': batch, 'ei': ei, 'W': W}
    _L3_gnn_all = _L3_gnn_setup()
    _L3_gnn_in = {k: v for k, v in _L3_gnn_all.items() if k in ('W',)}
    del _L3_gnn_all
    return {'x': x, 'src': src, 'dst': dst, 'edge_type_8': edge_type_8, 'edge_weight': edge_weight, 'L0_gnn_ln_gamma': _L0_gnn_in['ln_gamma'], 'L0_gnn_ln_beta': _L0_gnn_in['ln_beta'], 'L0_gnn_w_l': _L0_gnn_in['w_l'], 'L0_gnn_b_l': _L0_gnn_in['b_l'], 'L0_gnn_w_r': _L0_gnn_in['w_r'], 'L1_gnn_Wq': _L1_gnn_in['Wq'], 'L1_gnn_Wk': _L1_gnn_in['Wk'], 'L1_gnn_Wv': _L1_gnn_in['Wv'], 'L1_gnn_Wo': _L1_gnn_in['Wo'], 'L1_gnn_ln1_g': _L1_gnn_in['ln1_g'], 'L1_gnn_ln1_b': _L1_gnn_in['ln1_b'], 'L1_gnn_ln2_g': _L1_gnn_in['ln2_g'], 'L1_gnn_ln2_b': _L1_gnn_in['ln2_b'], 'L1_gnn_W1': _L1_gnn_in['W1'], 'L1_gnn_b1': _L1_gnn_in['b1'], 'L1_gnn_W2': _L1_gnn_in['W2'], 'L1_gnn_b2': _L1_gnn_in['b2'], 'L2_gnn_W': _L2_gnn_in['W'], 'L2_gnn_a_src': _L2_gnn_in['a_src'], 'L2_gnn_a_dst': _L2_gnn_in['a_dst'], 'L2_gnn_et_emb': _L2_gnn_in['et_emb'], 'L2_gnn_ln_gamma': _L2_gnn_in['ln_gamma'], 'L2_gnn_ln_beta': _L2_gnn_in['ln_beta'], 'L3_gnn_W': _L3_gnn_in['W']}

def reference(x, src, dst, edge_type_8, edge_weight, L0_gnn_ln_gamma, L0_gnn_ln_beta, L0_gnn_w_l, L0_gnn_b_l, L0_gnn_w_r, L1_gnn_Wq, L1_gnn_Wk, L1_gnn_Wv, L1_gnn_Wo, L1_gnn_ln1_g, L1_gnn_ln1_b, L1_gnn_ln2_g, L1_gnn_ln2_b, L1_gnn_W1, L1_gnn_b1, L1_gnn_W2, L1_gnn_b2, L2_gnn_W, L2_gnn_a_src, L2_gnn_a_dst, L2_gnn_et_emb, L2_gnn_ln_gamma, L2_gnn_ln_beta, L3_gnn_W):
    import jax
    import jax.numpy as jnp

    def _L0_gnn_ref(node_feature, edge_index, ln_gamma, ln_beta, w_l, b_l, w_r):
        import jax, jax.numpy as jnp
        import numpy as np
        LN_EPS = 1e-05
        N = node_feature.shape[0]
        residual = node_feature
        mu = jnp.mean(node_feature, axis=-1, keepdims=True)
        var = jnp.mean(jnp.square(node_feature - mu), axis=-1, keepdims=True)
        x = (node_feature - mu) * jax.lax.rsqrt(var + LN_EPS) * ln_gamma + ln_beta
        src, dst = (edge_index[0], edge_index[1])
        msg = x[src]
        summed = jax.ops.segment_sum(msg, dst, num_segments=N)
        cnt = jax.ops.segment_sum(jnp.ones_like(dst, dtype=x.dtype), dst, num_segments=N)
        agg = summed / jnp.maximum(cnt, 1.0)[:, None]
        out = agg @ w_l.T + b_l + x @ w_r.T
        out = jax.nn.relu(out)
        return out + residual

    def _L1_gnn_ref(h, src, dst, Wq, Wk, Wv, Wo, ln1_g, ln1_b, ln2_g, ln2_b, W1, b1, W2, b2):
        import jax, jax.numpy as jnp
        import numpy as np
        N, E, DM, H, DFF = (625, 20000, 512, 8, 64)
        DK = DM // H

        def _layernorm(x, g, b, eps=1e-05):
            mu = jnp.mean(x, axis=-1, keepdims=True)
            var = jnp.mean(jnp.square(x - mu), axis=-1, keepdims=True)
            return (x - mu) * jax.lax.rsqrt(var + eps) * g + b
        n = h.shape[0]
        q = (h @ Wq).reshape(n, H, DK)
        k = (h @ Wk).reshape(n, H, DK)
        v = (h @ Wv).reshape(n, H, DK)
        e = jnp.einsum('ehd,ehd->eh', k[src], q[dst]) / np.sqrt(DK).astype(np.float32)
        m = jax.ops.segment_max(e, dst, num_segments=n)
        ex = jnp.exp(e - m[dst])
        z = jax.ops.segment_sum(ex, dst, num_segments=n)
        attn = ex / z[dst]
        a = jax.ops.segment_sum(attn[:, :, None] * v[src], dst, num_segments=n)
        a = a.reshape(n, DM)
        o = a @ Wo
        x = _layernorm(h + o, ln1_g, ln1_b)
        f = jax.nn.relu(x @ W1 + b1) @ W2 + b2
        return _layernorm(x + f, ln2_g, ln2_b)

    def _L2_gnn_ref(x, edge_index, edge_type, edge_weight, W, a_src, a_dst, et_emb, ln_gamma, ln_beta):
        import jax, jax.numpy as jnp
        import numpy as np
        N, IN_DIM, H, D, E = (50000, 512, 8, 64, 25000)
        NEG_SLOPE = 0.2
        LN_EPS = 1e-05
        n, h_, d_ = (x.shape[0], a_src.shape[0], a_src.shape[1])
        h = (x @ W.T).reshape(n, h_, d_)
        src, dst = (edge_index[0], edge_index[1])
        h_src = h[src]
        e_src = jnp.einsum('ehd,hd->eh', h_src, a_src)
        e_dst = jnp.einsum('ehd,hd->eh', h[dst], a_dst)
        e = jax.nn.leaky_relu(e_src + e_dst, NEG_SLOPE)
        e = e * (1.0 + et_emb[edge_type])
        e = e * edge_weight[:, None]
        e_max = jnp.zeros((n, h_), x.dtype).at[dst].max(e)
        e = jnp.exp(e - e_max[dst])
        e_sum = jnp.zeros((n, h_), x.dtype).at[dst].add(e)
        alpha = e / (e_sum[dst] + 1e-10)
        msg = h_src * alpha[:, :, None]
        out = jnp.zeros((n, h_, d_), x.dtype).at[dst].add(msg).reshape(n, h_ * d_)
        out = out + x
        mu = jnp.mean(out, axis=-1, keepdims=True)
        var = jnp.var(out, axis=-1, keepdims=True)
        return (out - mu) / jnp.sqrt(var + LN_EPS) * ln_gamma + ln_beta

    def _L3_gnn_ref(x, batch, ei, W):
        import jax, jax.numpy as jnp
        import numpy as np
        N = 625
        E = 250000
        B = 128
        Fin = 512
        Fqk = 512
        Fv = 512
        H = 8
        src, dest = (ei[0], ei[1])
        n = x.shape[0]
        Fh = Fqk // H
        Fhv = Fv // H
        scaling = float(Fh) ** (-0.5)
        qkv = x @ W
        q, k, v = jnp.split(qkv, [Fqk, 2 * Fqk], axis=-1)
        q = (q * scaling).reshape(n, H, Fh)
        k = k.reshape(n, H, Fh)
        v = v.reshape(n, H, Fhv)
        qs = q[src]
        ks = k[dest]
        vs = v[dest]
        aw = jnp.einsum('ehf,ehf->eh', qs, ks)
        m = jax.ops.segment_max(aw, src, num_segments=n)
        e = jnp.exp(aw - m[src])
        denom = jax.ops.segment_sum(e, src, num_segments=n)
        alpha = e / denom[src]
        out = jax.ops.segment_sum(alpha[:, :, None] * vs, src, num_segments=n)
        return out.reshape(n, Fv)
    edge_index = jnp.stack([src, dst])
    batch0 = jnp.zeros((10000,), jnp.int32)
    x = _layernorm(x + _L0_gnn_ref(x, edge_index, L0_gnn_ln_gamma, L0_gnn_ln_beta, L0_gnn_w_l, L0_gnn_b_l, L0_gnn_w_r), axis=-1)
    x = _layernorm(x + _L1_gnn_ref(x, src, dst, L1_gnn_Wq, L1_gnn_Wk, L1_gnn_Wv, L1_gnn_Wo, L1_gnn_ln1_g, L1_gnn_ln1_b, L1_gnn_ln2_g, L1_gnn_ln2_b, L1_gnn_W1, L1_gnn_b1, L1_gnn_W2, L1_gnn_b2), axis=-1)
    x = _layernorm(x + _L2_gnn_ref(x, edge_index, edge_type_8, edge_weight, L2_gnn_W, L2_gnn_a_src, L2_gnn_a_dst, L2_gnn_et_emb, L2_gnn_ln_gamma, L2_gnn_ln_beta), axis=-1)
    x = _layernorm(x + _L3_gnn_ref(x, batch0, edge_index, L3_gnn_W), axis=-1)
    return x

_drawn_inputs = setup_inputs


def setup_inputs(seed=0):
    import zlib

    import numpy as np

    out = dict(_drawn_inputs(seed))
    spreads = {'L0_gnn_ln_gamma': (1.0, 0.2),
     'L0_gnn_ln_beta': (0.0, 0.1),
     'L0_gnn_b_l': (0.0, 0.1),
     'L1_gnn_ln1_g': (1.0, 0.2),
     'L1_gnn_ln1_b': (0.0, 0.1),
     'L1_gnn_ln2_g': (1.0, 0.2),
     'L1_gnn_ln2_b': (0.0, 0.1),
     'L1_gnn_b1': (0.0, 0.8),
     'L1_gnn_b2': (0.0, 0.1),
     'L2_gnn_ln_gamma': (1.0, 0.2),
     'L2_gnn_ln_beta': (0.0, 0.1)}
    factors = {'L1_gnn_Wq': 8.0, 'L1_gnn_Wk': 8.0}
    for name, (base, spread) in spreads.items():
        noise = np.random.default_rng([zlib.crc32(name.encode()), seed]).standard_normal(out[name].shape)
        drawn = base * np.exp(spread * noise) if base else spread * noise
        out[name] = jnp.asarray(drawn.astype(out[name].dtype))
    for name, factor in factors.items():
        out[name] = (out[name] * factor).astype(out[name].dtype)
    return out
```

```python
from contextlib import ExitStack, contextmanager

import numpy as np

import concourse.bass as bass
from concourse import mybir

F32 = mybir.dt.float32
F32R = mybir.dt.float32r
BF16 = mybir.dt.bfloat16
I32 = mybir.dt.int32
ACT = mybir.ActivationFunctionType
ALU = mybir.AluOpType
X = mybir.AxisListType.X

P = 128
N, D, E = 10000, 512, 5000
H, DH, DFF, NTYPE = 8, 64, 64, 8
KC = D // P
NT = 80
NP = NT * P
EC = 125
ET = E // EC
SLOTS = ET * P
PER = P - 1
EPS = 1e-5
FAR = -1e30
MAGIC = float(3 << 22)
SRC, DST, TYP, WGT = 0, 1, 2, 3

assert NP >= N + P and ET * PER >= E and SLOTS == ET * P and KC * P == D
assert D == H * DH and EC * ET == E


def host_constants():
    j = np.arange(P, dtype=np.float32)
    iota = np.tile(j, (P, 1))
    part = iota.T
    c = {
        "iota": iota,
        "ident": (iota == part).astype(np.float32),
        "earlier": (iota < part).astype(np.float32),
        "above": (iota > part).astype(np.float32),
        "ones": np.ones((P, P), np.float32),
        "zrow": iota + SLOTS,
    }
    heads = np.zeros((P, KC, H), np.float32)
    for k in range(KC):
        for p in range(P):
            heads[p, k, (k * P + p) // DH] = 1.0
    table = np.zeros((SLOTS, 4), np.float32)
    table[:, SRC] = table[:, DST] = N
    eps = np.full((P, 1), EPS, np.float32)
    packed = np.concatenate([c[k] for k in CONSTS] + [heads.reshape(P, KC * H), part[:, :1], eps], axis=1)
    return np.ascontiguousarray(packed), table


CONSTS = ("iota", "ident", "earlier", "above", "ones", "zrow")
CW = len(CONSTS) * P + KC * H + 2


class Names:
    pass


class Tile:

    def __init__(self, i, b):
        self.i, self.b, self.m = i, b, i * 4 + b

    def back(self, lag):
        return Tile(self.i, self.b - lag)

    def known(self):
        return isinstance(self.i, int)

    def exists(self, count):
        return not self.known() or 0 <= self.m < count

    def slot(self, ring):
        return self.b % ring

    def turn(self, ring):
        return self.i * (4 // ring) + self.b // ring

    def reuses(self, ring):
        return not self.known() or self.m >= ring


def tiles(eng, count, lag, body):
    for b in range(4):
        body(Tile(0, b))
    with eng.Fori(1, count // 4) as i:
        for b in range(4):
            body(Tile(i, b))
    for b in range(lag):
        body(Tile(count // 4, b))


class Steps:

    def __init__(self, eng, sem, per):
        self.eng, self.sem, self.per = eng, sem, per

    def tile(self, m):
        self.base, self.k = m * self.per, 0
        return self

    def __call__(self, ins):
        self.last(ins)
        self.eng.wait_ge(self.sem, self.base + self.k)

    def alone(self, ins, passed):
        self(ins)
        self.eng.sem_inc(passed, 1)

    def last(self, ins):
        self.k += 1
        assert self.k <= self.per
        ins.then_inc(self.sem, 1)


@contextmanager
def phase(nc, name):
    with ExitStack() as ctx:
        f = Names()
        f.sems = []

        def sb(n, shape, dt=F32):
            return ctx.enter_context(nc.sbuf_tensor(f"{name}_{n}", shape, dt))

        def psum(n, shape, dt=F32):
            return ctx.enter_context(nc.psum_tensor(f"{name}_ps_{n}", shape, dt))

        def sem(n):
            s = nc.alloc_semaphore(f"{name}_{n}")
            f.sems.append(s)
            return s

        f.sb, f.psum, f.sem = sb, psum, sem
        f.passed_dve, f.passed_pool = sem("passed_dve"), sem("passed_pool")
        with nc.Block() as block:
            f.block = block
            yield f
        nc.clear_and_free_semaphores(f.sems)
        nc.all_engine_barrier()


def rows(ap, m):
    return ap[bass.ts(m, P), :]



def load_constants(nc, s):
    with phase(nc, "const") as f:
        loaded, zeroed, stored = f.sem("loaded"), f.sem("zeroed"), f.sem("stored")
        zeros = f.sb("zeros", [P, D])

        @f.block.sync
        def _(sp):
            sp.dma_start(s.packed[:], s.inputs["consts_dram"]).then_inc(loaded, 16)
            sp.wait_ge(zeroed, 1)
            sp.dma_start(s.edge_out[SLOTS:SLOTS + P, :], zeros[:]).then_inc(stored, 16)
            sp.wait_ge(loaded, 16)
            sp.wait_ge(stored, 16)

        @f.block.vector
        def _(dve):
            nc.vector.memset(zeros[:], 0.0).then_inc(zeroed, 1)


def sort_edges(nc, s, order):
    key = order.key
    G = 4
    with phase(nc, f"sort{key}") as f:
        raw = f.sb("raw", [EC, 3, ET], I32)
        pay = f.sb("pay", [EC, ET, 4])
        weight = f.sb("weight", [EC, ET])
        krow = f.sb("krow", [P, E], I32)
        hirow = f.sb("hirow", [P, E], I32)
        hi_onehot_t = f.sb("hi_onehot_t", [P, E])
        krow_f = f.sb("krow_f", [P, E])
        same = f.sb("same", [EC, E])
        hi_onehot = f.sb("hi_onehot", [EC, ET * P], BF16)
        lo_onehot = f.sb("lo_onehot", [EC, ET * P], BF16)
        digit = f.sb("digit", [EC, 2, ET], I32)
        digit_f = f.sb("digit_f", [EC, 2, ET])
        scan = f.sb("scan", [P, P])
        rowbase = f.sb("rowbase", [P, 1])
        end = f.sb("end", [P, P])
        base = f.sb("base", [P, P])
        table = f.sb("table", [P, 2, P])
        prod = f.sb("prod", [EC, 2, G * P])
        rank = f.sb("rank", [EC, ET])
        tie = f.sb("tie", [EC, ET])
        tmp = f.sb("tmp", [P, 3, P])
        slot_i = f.sb("slot_i", [EC, ET], I32)
        stage_slot = f.sb("stage_slot", [EC, 2], I32)
        stage_pay = f.sb("stage_pay", [EC, 2, 4])
        sorted_col = f.sb("sorted_col", [P, ET, 4])
        kout = f.sb("kout", [ET, P])
        kin = f.sb("kin", [ET, P])
        breaks = f.sb("breaks", [ET, P])
        begin = f.sb("begin", [1, 1])
        ps_total = f.psum("total", [P, 512])
        ps_small = f.psum("small", [P, 512])
        ps_place = f.psum("place", [P, 512])
        ps_key = f.psum("key", [P, 512])
        ps_run = f.psum("run", [P, 512])
        ps_look = [f.psum(f"look{b}", [EC, 512]) for b in range(2)]

        loads, prefilled = f.sem("loads"), f.sem("prefilled")
        cols_ready, total_ready, scanned, rowbase_ready = (
            f.sem("cols_ready"), f.sem("total_ready"), f.sem("scanned"), f.sem("rowbase_ready"))
        onehot_t_ready, table_ready, counted, looked = (
            f.sem("onehot_t_ready"), f.sem("table_ready"), f.sem("counted"), f.sem("looked"))
        summed, places_ready, places_turned = f.sem("summed"), f.sem("places_ready"), f.sem("places_turned")
        slots_ready, staged, sorted_loaded = f.sem("slots_ready"), f.sem("staged"), f.sem("sorted_loaded")
        scattered = [f.sem(f"scattered{b}") for b in range(2)]
        key_turned, kout_ready, kin_written = f.sem("key_turned"), f.sem("kout_ready"), f.sem("kin_written")
        kin_loaded, breaks_ready, written = f.sem("kin_loaded"), f.sem("breaks_ready"), f.sem("written")
        kin_turned = f.sem("kin_turned")
        picked = f.sem("picked")
        chain = f.sem("chain")

        @f.block.sync
        def _(sp):
            sp.dma_start(raw[:, 0, :], s.inputs["src_col"]).then_inc(loads, 16)
            sp.dma_start(raw[:, 1, :], s.inputs["dst_col"]).then_inc(loads, 16)
            sp.dma_start(raw[:, 2, :], s.inputs["type_col"]).then_inc(loads, 16)
            sp.dma_start(weight[:], s.inputs["weight_col"]).then_inc(loads, 16)
            sp.dma_start(krow[:], (s.inputs["dst_flat"] if key == DST else s.inputs["src_flat"]).partition_broadcast(P)).then_inc(loads, 16)
            sp.dma_start(order.table, s.inputs["table_default"]).then_inc(prefilled, 16)
            for b in range(2):
                sp.wait_ge(scattered[b], 16 * (ET // 2))
            sp.dma_start(sorted_col[:], order.table.rearrange("(t p) c -> p t c", p=P)).then_inc(sorted_loaded, 16)
            sp.wait_ge(kout_ready, 2)
            sp.dma_start(order.key_out.rearrange("(t p) -> t p", p=P), kout[:]).then_inc(written, 16)
            sp.dma_start(order.key_in[1:, 0:1], kout[0:ET - 1, P - 1:P], allow_slow_non_contiguous=True).then_inc(kin_written, 16)
            sp.dma_start(order.key_in[0:1, 0:1], begin[:]).then_inc(kin_written, 16)
            sp.dma_start(order.key_in[:, 1:P], kout[:, 1:P]).then_inc(kin_written, 16)
            sp.wait_ge(kin_written, 48)
            sp.dma_start(kin[:], order.key_in).then_inc(kin_loaded, 16)
            sp.wait_ge(breaks_ready, 2)
            sp.dma_start(order.breaks, breaks[:]).then_inc(written, 16)
            sp.wait_ge(written, 32)
            sp.wait_ge(kin_loaded, 16)
            sp.wait_ge(prefilled, 16)

        def look_sum(dve, g):
            dve.wait_ge(looked, (g + 1) * G)
            if g >= 2:
                dve.wait_ge(summed, g - 1)
            nc.vector.tensor_tensor(prod[:, g % 2, :], ps_look[g % 2][:], lo_onehot[:, bass.ts(g, G * P)], ALU.mult).then_inc(picked, 1)
            dve.wait_ge(picked, g + 1)
            nc.vector.tensor_reduce(rank[:, g * G:g * G + G], prod[:, g % 2, :].rearrange("p (t j) -> p t j", j=P),
                                    X, ALU.add).then_inc(summed, 1)

        @f.block.vector
        def _(dve):
            n = [0]

            def link(ins):
                n[0] += 1
                ins.then_inc(chain, 1)
                dve.wait_ge(chain, n[0])

            def slot_of(out, rank_ap, p, n):
                a, b = tmp[0:p, 1, 0:n], tmp[0:p, 2, 0:n]
                link(nc.vector.tensor_scalar(a, rank_ap, 0.5, 1.0 / PER, ALU.add, ALU.mult))
                link(nc.vector.tensor_scalar(b, a, -0.5, None, ALU.add))
                link(nc.vector.tensor_scalar(a, b, MAGIC, None, ALU.add))
                link(nc.vector.tensor_scalar(b, a, MAGIC, 1.0, ALU.subtract, ALU.add))
                link(nc.vector.tensor_tensor(out, rank_ap, b, ALU.add))

            dve.wait_ge(loads, 80)
            kcol = raw[:, key, :]
            link(nc.vector.tensor_scalar(digit[:, 0, :], kcol, 7, None, ALU.logical_shift_right))
            link(nc.vector.tensor_scalar(digit[:, 1, :], kcol, P - 1, None, ALU.bitwise_and))
            link(nc.vector.tensor_copy(digit_f[:], digit[:]))
            wide = [EC, ET, P]
            for g, onehot in ((0, hi_onehot), (1, lo_onehot)):
                nc.vector.tensor_tensor(
                    onehot[:].rearrange("p (t j) -> p t j", j=P), s.iota[0:EC, :].unsqueeze(1).to_broadcast(wide),
                    digit_f[:, g, :].unsqueeze(2).to_broadcast(wide), ALU.is_equal).then_inc(cols_ready, 1)
            for c in (SRC, DST, TYP):
                link(nc.vector.tensor_copy(pay[:, :, c], raw[:, c, :]))
            link(nc.vector.tensor_copy(pay[:, :, WGT], weight[:]))
            link(nc.vector.tensor_scalar(hirow[:], krow[:], 7, None, ALU.logical_shift_right))
            nc.vector.tensor_scalar(hi_onehot_t[:], hirow[:], s.part, None, ALU.is_equal).then_inc(onehot_t_ready, 1)
            link(nc.vector.tensor_copy(krow_f[:], krow[:]))

            dve.wait_ge(total_ready, 1)
            nc.vector.tensor_tensor_scan(scan[:], s.ones, ps_total[:, 0:P], 0.0, ALU.mult, ALU.add).then_inc(scanned, 1)
            dve.wait_ge(rowbase_ready, 1)
            link(nc.vector.tensor_copy(rowbase[:], ps_small[:, 0:1]))
            dve.wait_ge(scanned, 1)
            link(nc.vector.tensor_scalar(end[:], scan[:], rowbase[:], None, ALU.add))
            link(nc.vector.tensor_tensor(base[:], end[:], ps_total[:, 0:P], ALU.subtract))

            for g in range(ET // G):
                for t in range(g * G, g * G + G):
                    if t >= 2:
                        dve.wait_ge(looked, t - 1)
                    if t == 0:
                        nc.vector.tensor_copy(table[:, 0, :], base[:]).then_inc(table_ready, 1)
                    else:
                        dve.wait_ge(counted, t)
                        nc.vector.tensor_tensor(table[:, t % 2, :], base[:], ps_run[:, 0:P], ALU.add).then_inc(table_ready, 1)
                if g >= 1:
                    look_sum(dve, g - 1)
            look_sum(dve, ET // G - 1)

            cube = [EC, ET, EC]
            same3 = same[:].rearrange("p (t j) -> p t j", j=EC)
            kcol_f = pay[:, :, key].unsqueeze(2).to_broadcast(cube)
            link(nc.vector.tensor_tensor(same3, krow_f[0:EC, :].rearrange("p (t j) -> p t j", j=EC), kcol_f, ALU.is_equal))
            link(nc.vector.tensor_tensor(same3, same3, s.earlier[0:EC, 0:EC].unsqueeze(1).to_broadcast(cube), ALU.mult))
            link(nc.vector.tensor_reduce(tie[:], same3, X, ALU.add))
            dve.wait_ge(summed, ET // G)
            link(nc.vector.tensor_tensor(rank[:], rank[:], tie[:], ALU.add))
            slot_of(tmp[0:EC, 0, 0:ET], rank[:], EC, ET)
            nc.vector.tensor_copy(slot_i[:], tmp[0:EC, 0, 0:ET]).then_inc(slots_ready, 1)
            dve.wait_ge(slots_ready, 1)

            last = scan[:]
            link(nc.vector.tensor_scalar(last, end[:], -1.0, None, ALU.add))
            slot_of(tmp[:, 0, :], last, P, P)
            link(nc.vector.tensor_tensor(tmp[:, 0, :], tmp[:, 0, :], s.zrow, ALU.subtract))
            link(nc.vector.tensor_scalar(tmp[:, 1, :], ps_total[:, 0:P], 0.0, None, ALU.is_gt))
            link(nc.vector.tensor_tensor(tmp[:, 0, :], tmp[:, 0, :], tmp[:, 1, :], ALU.mult))
            nc.vector.tensor_tensor(tmp[:, 2, :], tmp[:, 0, :], s.zrow, ALU.add).then_inc(places_ready, 1)
            dve.wait_ge(places_turned, 1)
            link(nc.vector.tensor_copy(order.place[:], ps_place[:, 0:NT]))

            dve.wait_ge(sorted_loaded, 16)
            other = SRC + DST - key
            link(nc.vector.tensor_copy(order.other_idx[:], sorted_col[:, :, other]))
            link(nc.vector.tensor_copy(order.key_idx[:], sorted_col[:, :, key]))
            link(nc.vector.tensor_copy(order.type_col[:], sorted_col[:, :, TYP]))
            link(nc.vector.tensor_copy(order.weight_col[:], sorted_col[:, :, WGT]))
            nc.vector.memset(begin[:], -1.0).then_inc(kout_ready, 1)
            dve.wait_ge(key_turned, 1)
            link(nc.vector.tensor_copy(kout[:], ps_key[0:ET, 0:P]))
            nc.vector.tensor_copy(kout[:, 0:1], kout[:, P - 1:P]).then_inc(kout_ready, 1)
            dve.wait_ge(kin_loaded, 16)
            nc.vector.memset(breaks[:, 0:1], 0.0).then_inc(breaks_ready, 1)
            link(nc.vector.tensor_tensor(breaks[:, 1:P], kin[:, 1:P], kin[:, 0:P - 1], ALU.not_equal))
            nc.vector.tensor_scalar(breaks[:, 1:P], breaks[:, 1:P], FAR, None, ALU.mult).then_inc(breaks_ready, 1)
            dve.wait_ge(kin_turned, 1)
            link(nc.vector.tensor_copy(order.key_in_col[:], ps_small[:, 0:ET]))


        @f.block.tensor
        def _(pe):
            pe.wait_ge(cols_ready, 2)
            for t in range(ET):
                mm = pe.matmul(ps_total[:, 0:P], hi_onehot[:, bass.ts(t, P)], lo_onehot[:, bass.ts(t, P)],
                               start=t == 0, stop=t == ET - 1)
            mm.then_inc(total_ready, 1)
            pe.wait_ge(scanned, 1)
            pe.matmul(ps_small[:, 0:1], s.above, scan[:, P - 1:P], start=True, stop=True).then_inc(rowbase_ready, 1)
            pe.wait_ge(onehot_t_ready, 1)
            for t in range(ET):
                g = t // G
                pe.wait_ge(table_ready, t + 1)
                if t < ET - 1:
                    pe.matmul(ps_run[:, 0:P], hi_onehot[:, bass.ts(t, P)], lo_onehot[:, bass.ts(t, P)],
                              start=t == 0, stop=True, skip_group_check=True).then_inc(counted, 1)
                if g >= 2 and t % G == 0:
                    pe.wait_ge(picked, g - 1)
                pe.matmul(ps_look[g % 2][:, bass.ts(t % G, P)], hi_onehot_t[:, bass.ts(t, EC)], table[:, t % 2, :],
                          start=True, stop=True).then_inc(looked, 1)
            pe.wait_ge(places_ready, 1)
            pe.transpose(ps_place[:, 0:P], tmp[:, 2, :], s.ident).then_inc(places_turned, 1)
            pe.wait_ge(sorted_loaded, 16)
            pe.transpose(ps_key[0:ET, 0:P], sorted_col[:, :, key], s.ident).then_inc(key_turned, 1)
            pe.wait_ge(kin_loaded, 16)
            pe.transpose(ps_small[:, 0:ET], kin[:], s.ident[0:ET, 0:ET]).then_inc(kin_turned, 1)

        @f.block.gpsimd
        def _(pool):
            pool.wait_ge(slots_ready, 1)
            pool.wait_ge(prefilled, 16)
            with pool.Fori(0, ET // 2) as i:
                for b in range(2):
                    pool.wait_ge(scattered[b], i * 16)
                    nc.gpsimd.tensor_copy(stage_slot[:, b:b + 1], slot_i[:, bass.ds(i * 2 + b, 1)]).then_inc(staged, 1)
                    nc.gpsimd.tensor_copy(stage_pay[:, b, :], pay[:].rearrange("p t c -> p (t c)")[:, bass.ts(i * 2 + b, 4)]).then_inc(staged, 1)
                    pool.wait_ge(staged, i * 4 + 2 * b + 2)
                    pool.sem_inc(f.passed_pool, 1)
                    nc.gpsimd.indirect_dma_start(
                        out=order.table, out_offset=bass.IndirectOffsetOnAxis(ap=stage_slot[:, b:b + 1], axis=0),
                        in_=stage_pay[:, b, :], in_offset=None).then_inc(scattered[b], 16)



class Weights:

    def __init__(self, f, named, scales=None):
        self.named, self.scales = named, scales or {}
        self.stage = f.sb("w_stage", [P, 2, KC * D])
        self.hi = {k: f.sb(f"{k}_hi", [P, KC * w], F32R) for k, (_, w) in named.items()}
        self.lo = {k: f.sb(f"{k}_lo", [P, KC * w], F32R) for k, (_, w) in named.items()}
        self.loaded = [f.sem(f"w_loaded{b}") for b in range(2)]
        self.scaled, self.hi_done, self.lo_done = f.sem("w_scaled"), f.sem("w_hi"), f.sem("w_lo")
        self.count = len(named)

    def load(self, sp):
        for j, (src, w) in enumerate(self.named.values()):
            if j >= 2:
                sp.wait_ge(self.lo_done, j - 1)
            sp.dma_start(self.stage[:, j % 2, 0:KC * w].rearrange("p (k n) -> p k n", n=w),
                         src.rearrange("(k p) n -> p k n", p=P)).then_inc(self.loaded[j % 2], 16)

    def split_hi(self, nc, act):
        for j, (name, (_, w)) in enumerate(self.named.items()):
            act.wait_ge(self.loaded[j % 2], 16 * (j // 2 + 1))
            if self.scales:
                act.wait_ge(self.scaled, KC * (j + 1))
            nc.scalar.activation(self.hi[name][:], self.stage[:, j % 2, 0:KC * w], ACT.Copy).then_inc(self.hi_done, 1)

    def split_lo(self, nc, dve):
        for j, (name, (_, w)) in enumerate(self.named.items()):
            stage = self.stage[:, j % 2, 0:KC * w]
            if self.scales:
                dve.wait_ge(self.loaded[j % 2], 16 * (j // 2 + 1))
                for k in range(KC):
                    nc.vector.tensor_scalar(stage[:, bass.ts(k, w)], stage[:, bass.ts(k, w)],
                                            self.scales[name][:, k:k + 1], None, ALU.mult).then_inc(self.scaled, 1)
            dve.wait_ge(self.hi_done, j + 1)
            nc.vector.tensor_tensor(self.lo[name][:], stage, self.hi[name][:].bitcast(F32), ALU.subtract).then_inc(self.lo_done, 1)

    def product(self, pe, out, hi, lo, name):
        w = self.named[name][1]
        for k in range(KC):
            for j, (a, b) in enumerate(((hi, self.hi), (hi, self.lo), (lo, self.hi))):
                mm = pe.matmul(out, a[:, bass.ts(k, P)], b[name][:, bass.ts(k, w)],
                               start=k == 0 and j == 0, stop=k == KC - 1 and j == 2)
        return mm


def transpose_tile(pe, out, tile, ident):
    for k in range(KC):
        mm = pe.transpose(out[:, bass.ts(k, P)], tile[:, bass.ts(k, P)], ident)
    return mm


def norm_stats(nc, steps, passed, stats, mv, x):
    steps.alone(nc.vector.bn_stats(stats, x), passed)
    steps.last(nc.vector.bn_aggr(mv, stats))


def deviation(nc, s, out, mv):
    return nc.scalar.activation(out, mv[:, 1:2], ACT.Sqrt, bias=s.eps)


def norm_scale(nc, steps, mv, dev, rstd):
    steps(nc.vector.reciprocal(rstd[:, 0:1], dev))
    steps.last(nc.vector.tensor_scalar(rstd[:, 1:2], mv[:, 0:1], rstd[:, 0:1], -1.0, ALU.mult, ALU.mult))


def gather(nc, pool, passed, staged, t, idx, stage, table, out, done):
    nc.gpsimd.tensor_copy(stage, idx[:, bass.ds(t.m, 1)]).then_inc(staged[0], 1)
    pool.wait_ge(staged[0], t.m * staged[1] + staged[2])
    pool.sem_inc(passed, 1)
    nc.gpsimd.indirect_dma_start(out=out, out_offset=None, in_=table,
                                 in_offset=bass.IndirectOffsetOnAxis(ap=stage, axis=0)).then_inc(done, 16)



def dense_root(nc, s):
    with phase(nc, "root") as f:
        gcol, bcol = f.sb("gcol", [P, KC]), f.sb("bcol", [P, KC])
        brows = f.sb("brows", [P, KC * P])
        bl = f.sb("bl", [P, D])
        wr_plain = f.sb("wr_plain", [P, KC * D])
        bias = f.sb("bias", [P, D])
        W = Weights(f, {"wr": (s.inputs["wr_t"], D)}, {"wr": gcol})
        x = f.sb("x", [P, 4, D])
        z = f.sb("z", [P, 2, D])
        hi, lo = f.sb("hi", [P, 2, D], F32R), f.sb("lo", [P, 2, D], F32R)
        u = f.sb("u", [P, 2, D])
        stats, mv, dev, rstd = f.sb("stats", [P, 2, 6]), f.sb("mv", [P, 2, 2]), f.sb("dev", [P, 2, 1]), f.sb("rstd", [P, 2, 1])
        dev_done = f.sem("dev_done")
        ps_t = [f.psum(f"t{b}", [P, D]) for b in range(2)]
        ps_o = [f.psum(f"o{b}", [P, D]) for b in range(2)]
        params, brows_ready, bias_made, bias_ready = f.sem("params"), f.sem("brows"), f.sem("bias_made"), f.sem("bias_ready")
        x_loaded = [f.sem(f"x_loaded{b}") for b in range(4)]
        u_stored = [f.sem(f"u_stored{b}") for b in range(2)]
        norm, turned, hi_done, lo_done, mm_done, u_ready = (f.sem(n) for n in (
            "norm", "turned", "hi_done", "lo_done", "mm_done", "u_ready"))

        @f.block.sync
        def _(sp):
            sp.dma_start(gcol[:], s.inputs["ln0_g_col"]).then_inc(params, 16)
            sp.dma_start(bcol[:], s.inputs["ln0_b_col"]).then_inc(params, 16)
            sp.dma_start(bl[:], s.inputs["b_l"].partition_broadcast(P)).then_inc(params, 16)
            sp.dma_start(wr_plain[:].rearrange("p (k n) -> p k n", n=D),
                         s.inputs["wr_t"].rearrange("(k p) n -> p k n", p=P)).then_inc(params, 16)
            W.load(sp)

            def step(t):
                if t.exists(NT):
                    if t.reuses(4):
                        sp.wait_ge(norm, 4 * (t.m - 3))
                    sp.dma_start(x[:, t.slot(4), :], rows(s.inputs["x"], t.m)).then_inc(x_loaded[t.slot(4)], 16)
                t = t.back(4)
                if t.exists(NT):
                    sp.wait_ge(u_ready, t.m + 1)
                    sp.dma_start(rows(s.root, t.m), u[:, t.slot(2), :]).then_inc(u_stored[t.slot(2)], 16)
            tiles(sp, NT, 4, step)
            for b in range(2):
                sp.wait_ge(u_stored[b], 16 * (NT // 2))

        @f.block.vector
        def _(dve):
            steps = Steps(dve, norm, 4)
            dve.wait_ge(params, 64)
            for k in range(KC):
                nc.vector.tensor_scalar(brows[:, bass.ts(k, P)], s.ones, bcol[:, k:k + 1], None, ALU.mult).then_inc(brows_ready, 1)
            W.split_lo(nc, dve)
            dve.wait_ge(bias_made, 1)
            nc.vector.tensor_tensor(bias[:], bl[:], ps_o[0][:], ALU.add).then_inc(bias_ready, 1)

            def step(t):
                if t.exists(NT):
                    b = t.slot(2)
                    xt = x[:, t.slot(4), :]
                    st = steps.tile(t.m)
                    dve.wait_ge(x_loaded[t.slot(4)], 16 * t.turn(4) + 16)
                    norm_stats(nc, st, f.passed_dve, stats[:, b, :], mv[:, b, :], xt)
                now = t
                t = t.back(1)
                if t.exists(NT):
                    b = t.slot(2)
                    dve.wait_ge(hi_done, t.m + 1)
                    nc.vector.tensor_tensor(lo[:, b, :], ps_t[b][:], hi[:, b, :].bitcast(F32), ALU.subtract).then_inc(lo_done, 1)
                t = t.back(1)
                if t.exists(NT):
                    b = t.slot(2)
                    dve.wait_ge(mm_done, t.m + 1)
                    if t.reuses(2):
                        dve.wait_ge(u_stored[b], 16 * t.turn(2))
                    else:
                        dve.wait_ge(bias_ready, 1)
                    nc.vector.tensor_tensor(u[:, b, :], ps_o[b][:], bias[:], ALU.add).then_inc(u_ready, 1)
                t = now
                if t.exists(NT):
                    b = t.slot(2)
                    dve.wait_ge(dev_done, t.m + 1)
                    st(nc.vector.reciprocal(rstd[:, b, :], dev[:, b, :]))
                    if t.reuses(2):
                        dve.wait_ge(turned, t.m - 1)
                    st.last(nc.vector.tensor_scalar(z[:, b, :], xt, mv[:, b, 0:1], rstd[:, b, :], ALU.subtract, ALU.mult))
            tiles(dve, NT, 2, step)

        @f.block.scalar
        def _(act):
            nc.scalar.preload_act_table(ACT.Sqrt)
            W.split_hi(nc, act)

            def step(t):
                if t.exists(NT):
                    b = t.slot(2)
                    act.wait_ge(norm, 4 * t.m + 2)
                    deviation(nc, s, dev[:, b, :], mv[:, b, :]).then_inc(dev_done, 1)
                    act.wait_ge(turned, t.m + 1)
                    if t.reuses(2):
                        act.wait_ge(mm_done, t.m - 1)
                    nc.scalar.activation(hi[:, b, :], ps_t[b][:], ACT.Copy).then_inc(hi_done, 1)
            tiles(act, NT, 0, step)

        @f.block.tensor
        def _(pe):
            pe.wait_ge(brows_ready, KC)
            for k in range(KC):
                mm = pe.matmul(ps_o[0][:], brows[:, bass.ts(k, P)], wr_plain[:, bass.ts(k, D)], start=k == 0, stop=k == KC - 1)
            mm.then_inc(bias_made, 1)
            pe.wait_ge(W.lo_done, W.count)
            pe.wait_ge(bias_ready, 1)

            def step(t):
                if t.exists(NT):
                    b = t.slot(2)
                    pe.wait_ge(norm, 4 * t.m + 4)
                    if t.reuses(2):
                        pe.wait_ge(lo_done, t.m - 1)
                    transpose_tile(pe, ps_t[b], z[:, b, :], s.ident).then_inc(turned, 1)
                t = t.back(1)
                if t.exists(NT):
                    b = t.slot(2)
                    pe.wait_ge(lo_done, t.m + 1)
                    if t.reuses(2):
                        pe.wait_ge(u_ready, t.m - 1)
                    W.product(pe, ps_o[b][:], hi[:, b, :], lo[:, b, :], "wr").then_inc(mm_done, 1)
            tiles(pe, NT, 1, step)



def aggregate(nc, s, order, name, values=None, weights=None, source=None, matrix=None, small=0.0):
    mean = source is not None
    ZW = 1 if mean else H
    with phase(nc, name) as f:
        key_out = f.sb("key_out", [P, SLOTS])
        v = f.sb("v", [P, 2, D + ZW])
        sel = f.sb("sel", [P, 2, P])
        a = f.sb("a", [P, 2, D])
        rz = f.sb("rz", [P, 2, 2 * H])
        zero = f.sb("zero", [1, D])
        ps_r = [f.psum(f"r{b}", [P, D]) for b in range(2)]
        ps_z = [f.psum(f"z{b}", [P, 512]) for b in range(2)]
        setup, zeroed = f.sem("setup"), f.sem("zeroed")
        v_steps, sel_ready, carried, summed = f.sem("v_steps"), f.sem("sel_ready"), f.sem("carried"), f.sem("summed")
        a_steps, turned, hi_done, lo_done, mm_done, o_ready = (f.sem(n) for n in (
            "a_steps", "turned", "hi_done", "lo_done", "mm_done", "o_ready"))
        stored = [f.sem(f"stored{b}") for b in range(2)]
        if mean:
            x = f.sb("x", [P, 4, D])
            stage = f.sb("stage", [P, 4], I32)
            stats, mv, dev, rstd = f.sb("stats", [P, 2, 6]), f.sb("mv", [P, 2, 2]), f.sb("dev", [P, 2, 1]), f.sb("rstd", [P, 2, 1])
            dev_done = f.sem("dev_done")
            gathered = [f.sem(f"gathered{b}") for b in range(4)]
            staged = f.sem("staged")
            gcol, bcol = f.sb("gcol", [P, KC]), f.sb("bcol", [P, KC])
            brows = f.sb("brows", [P, KC * P])
            plain = f.sb("plain", [P, KC * D])
            bias = f.sb("bias", [P, D])
            brows_ready, bias_made, bias_ready = f.sem("brows"), f.sem("bias_made"), f.sem("bias_ready")
        if matrix is not None:
            W = Weights(f, {"w": (matrix, D)}, {"w": gcol} if mean else None)
            hi, lo = f.sb("hi", [P, 2, D], F32R), f.sb("lo", [P, 2, D], F32R)
            o = f.sb("o", [P, 2, D])
            ps_t = [f.psum(f"t{b}", [P, D]) for b in range(2)]
            ps_o = [f.psum(f"o{b}", [P, D]) for b in range(2)]
        VS = 4 if mean else 2
        AS = 2 if small == 0.0 else 3
        out_lag = 4 if matrix is not None else 2

        @f.block.sync
        def _(sp):
            sp.dma_start(key_out[:], order.key_out.partition_broadcast(P)).then_inc(setup, 16)
            if mean:
                sp.dma_start(gcol[:], s.inputs["ln0_g_col"]).then_inc(setup, 16)
                sp.dma_start(bcol[:], s.inputs["ln0_b_col"]).then_inc(setup, 16)
                sp.dma_start(plain[:].rearrange("p (k n) -> p k n", n=D),
                             matrix.rearrange("(k p) n -> p k n", p=P)).then_inc(setup, 16)
            if matrix is not None:
                W.load(sp)

            def step(t):
                t = t.back(out_lag)
                if t.exists(ET):
                    b = t.slot(2)
                    if matrix is not None:
                        sp.wait_ge(o_ready, t.m + 1)
                        res = o[:, b, :]
                    else:
                        sp.wait_ge(a_steps, AS * t.m + AS)
                        res = a[:, b, :]
                    sp.dma_start(rows(s.edge_out, t.m), res).then_inc(stored[b], 16)
            tiles(sp, ET, out_lag, step)
            for b in range(2):
                sp.wait_ge(stored[b], 16 * (ET // 2))

        if mean:
            @f.block.gpsimd
            def _(pool):
                def step(t):
                    r = t.slot(4)
                    if t.reuses(4):
                        pool.wait_ge(v_steps, VS * (t.m - 3))
                        pool.wait_ge(gathered[r], 16 * t.turn(4))
                    gather(nc, pool, f.passed_pool, (staged, 1, 1), t, order.other_idx, stage[:, r:r + 1], source, x[:, r, :], gathered[r])
                tiles(pool, ET, 0, step)

        @f.block.vector
        def _(dve):
            vs, asteps = Steps(dve, v_steps, VS), Steps(dve, a_steps, AS)
            nc.vector.memset(zero[:], 0.0).then_inc(zeroed, 1)
            if mean:
                nc.vector.memset(v[:, :, D:D + 1], 1.0).then_inc(zeroed, 1)
                dve.wait_ge(setup, 64)
                for k in range(KC):
                    nc.vector.tensor_scalar(brows[:, bass.ts(k, P)], s.ones, bcol[:, k:k + 1], None, ALU.mult).then_inc(brows_ready, 1)
            if matrix is not None:
                W.split_lo(nc, dve)
            if mean:
                dve.wait_ge(bias_made, 1)
                nc.vector.tensor_copy(bias[:], ps_o[0][:]).then_inc(bias_ready, 1)
                dve.wait_ge(bias_ready, 1)

            def divide(t):
                if not t.exists(ET):
                    return
                b = t.slot(2)
                st = asteps.tile(t.m)
                z = ps_z[b][:, 0:ZW]
                dve.wait_ge(summed, t.m + 1)
                if not (t.known() and t.m == ET - 1):
                    dve.wait_ge(carried, 2 * t.m + 4)
                if small:
                    st(nc.vector.tensor_scalar(rz[:, b, H:H + ZW], z, small, None, ALU.add))
                    z = rz[:, b, H:H + ZW]
                st(nc.vector.reciprocal(rz[:, b, 0:ZW], z))
                if t.reuses(2):
                    if matrix is not None:
                        dve.wait_ge(turned, t.m - 1)
                    else:
                        dve.wait_ge(stored[b], 16 * t.turn(2))
                if mean:
                    st.last(nc.vector.tensor_scalar(a[:, b, :], ps_r[b][:], rz[:, b, 0:1], None, ALU.mult))
                else:
                    st.last(nc.vector.tensor_tensor(
                        a[:, b, :].rearrange("p (h d) -> p h d", d=DH), ps_r[b][:].rearrange("p (h d) -> p h d", d=DH),
                        rz[:, b, 0:H].unsqueeze(2).to_broadcast([P, H, DH]), ALU.mult))

            def step(t):
                now, before = t, t.back(1)
                if mean and now.exists(ET):
                    b = now.slot(2)
                    xt = x[:, now.slot(4), :]
                    st = vs.tile(now.m)
                    dve.wait_ge(gathered[now.slot(4)], 16 * now.turn(4) + 16)
                    norm_stats(nc, st, f.passed_dve, stats[:, b, :], mv[:, b, :], xt)
                if now.exists(ET):
                    b = now.slot(2)
                    if now.known() and now.m == 0:
                        dve.wait_ge(setup, 64 if mean else 16)
                    if mean:
                        dve.wait_ge(dev_done, now.m + 1)
                        st(nc.vector.reciprocal(rstd[:, b, :], dev[:, b, :]))
                        if now.reuses(2):
                            dve.wait_ge(summed, now.m - 1)
                        st.last(nc.vector.tensor_scalar(v[:, b, 0:D], xt, mv[:, b, 0:1], rstd[:, b, :], ALU.subtract, ALU.mult))
                    else:
                        st = vs.tile(now.m)
                        if now.reuses(2):
                            dve.wait_ge(summed, now.m - 1)
                        w = weights[:, bass.ts(now.m, H)]
                        st.last(nc.vector.tensor_tensor(
                            v[:, b, 0:D].rearrange("p (h d) -> p h d", d=DH), values[:, bass.ts(now.m, D)].rearrange("p (h d) -> p h d", d=DH),
                            w.unsqueeze(2).to_broadcast([P, H, DH]), ALU.mult))
                        st.last(nc.vector.tensor_copy(v[:, b, D:D + H], w))
                    nc.vector.tensor_scalar(sel[:, b, :], key_out[:, bass.ts(now.m, P)], order.key_in_col[:, bass.ds(now.m, 1)],
                                            None, ALU.is_equal).then_inc(sel_ready, 1)
                divide(before)
                t = before
                if matrix is None:
                    return
                t = t.back(1)
                if t.exists(ET):
                    b = t.slot(2)
                    dve.wait_ge(hi_done, t.m + 1)
                    nc.vector.tensor_tensor(lo[:, b, :], ps_t[b][:], hi[:, b, :].bitcast(F32), ALU.subtract).then_inc(lo_done, 1)
                t = t.back(1)
                if mean and t.exists(ET):
                    b = t.slot(2)
                    dve.wait_ge(mm_done, t.m + 1)
                    if t.reuses(2):
                        dve.wait_ge(stored[b], 16 * t.turn(2))
                    nc.vector.tensor_tensor(o[:, b, :], ps_o[b][:], bias[:], ALU.add).then_inc(o_ready, 1)
            tiles(dve, ET, 1 if matrix is None else 3, step)

        @f.block.scalar
        def _(act):
            if mean:
                nc.scalar.preload_act_table(ACT.Sqrt)
            if matrix is not None:
                W.split_hi(nc, act)

            def step(t):
                if mean and t.exists(ET):
                    b = t.slot(2)
                    act.wait_ge(v_steps, VS * t.m + 2)
                    deviation(nc, s, dev[:, b, :], mv[:, b, :]).then_inc(dev_done, 1)
                if t.exists(ET):
                    b, before = t.slot(2), t.back(1).slot(2)
                    act.wait_ge(v_steps, VS * t.m + VS)
                    if t.known() and t.m == 0:
                        act.wait_ge(zeroed, 2 if mean else 1)
                        r, z = zero[0:1, 0:D], zero[0:1, 0:ZW]
                    else:
                        act.wait_ge(summed, t.m)
                        r, z = ps_r[before][0:1, :], ps_z[before][0:1, 0:ZW]
                    nc.scalar.activation(v[0:1, b, 0:D], r, ACT.Copy).then_inc(carried, 1)
                    nc.scalar.activation(v[0:1, b, D:D + ZW], z, ACT.Copy).then_inc(carried, 1)
                if matrix is None:
                    return
                t = t.back(1)
                if t.exists(ET):
                    b = t.slot(2)
                    act.wait_ge(turned, t.m + 1)
                    if t.reuses(2):
                        act.wait_ge(mm_done, t.m - 1)
                    nc.scalar.activation(hi[:, b, :], ps_t[b][:], ACT.Copy).then_inc(hi_done, 1)
                t = t.back(2)
                if not mean and t.exists(ET):
                    b = t.slot(2)
                    act.wait_ge(mm_done, t.m + 1)
                    if t.reuses(2):
                        act.wait_ge(stored[b], 16 * t.turn(2))
                    nc.scalar.activation(o[:, b, :], ps_o[b][:], ACT.Copy).then_inc(o_ready, 1)
            tiles(act, ET, 0 if matrix is None else (1 if mean else 3), step)

        @f.block.tensor
        def _(pe):
            if mean:
                pe.wait_ge(setup, 64)
                pe.wait_ge(brows_ready, KC)
                for k in range(KC):
                    mm = pe.matmul(ps_o[0][:], brows[:, bass.ts(k, P)], plain[:, bass.ts(k, D)], start=k == 0, stop=k == KC - 1)
                mm.then_inc(bias_made, 1)
                pe.wait_ge(bias_ready, 1)
            if matrix is not None:
                pe.wait_ge(W.lo_done, W.count)

            def step(t):
                if t.exists(ET):
                    b = t.slot(2)
                    pe.wait_ge(sel_ready, t.m + 1)
                    pe.wait_ge(carried, 2 * t.m + 2)
                    if t.reuses(2):
                        pe.wait_ge(a_steps, AS * (t.m - 1))
                    pe.matmul(ps_r[b][:], sel[:, b, :], v[:, b, 0:D], start=True, stop=True)
                    pe.matmul(ps_z[b][:, 0:ZW], sel[:, b, :], v[:, b, D:D + ZW], start=True, stop=True).then_inc(summed, 1)
                if matrix is None:
                    return
                t = t.back(1)
                if t.exists(ET):
                    b = t.slot(2)
                    pe.wait_ge(a_steps, AS * t.m + AS)
                    if t.reuses(2):
                        pe.wait_ge(lo_done, t.m - 1)
                    transpose_tile(pe, ps_t[b], a[:, b, :], s.ident).then_inc(turned, 1)
                t = t.back(1)
                if t.exists(ET):
                    b = t.slot(2)
                    pe.wait_ge(lo_done, t.m + 1)
                    if t.reuses(2):
                        pe.wait_ge(o_ready, t.m - 1)
                    W.product(pe, ps_o[b][:], hi[:, b, :], lo[:, b, :], "w").then_inc(mm_done, 1)
            tiles(pe, ET, 0 if matrix is None else 2, step)



def edge_products(nc, s, order, name, table, w_other, w_key, values, scores, dots=None):
    attention = dots is None
    with phase(nc, name) as f:
        W = Weights(f, {**w_other, **w_key})
        xo, xk = f.sb("xo", [P, 2, D]), f.sb("xk", [P, 2, D])
        stage = f.sb("stage", [P, 4], I32)
        part = {(w, h): f.sb(f"x_{w}_{h}", [P, 2, D], F32R) for w in "ok" for h in ("hi", "lo")}
        ps_t = {(w, b): f.psum(f"t{w}{b}", [P, D]) for w in "ok" for b in range(2)}
        staged = f.sem("staged")
        g_other = [f.sem(f"g_other{b}") for b in range(2)]
        g_key = [f.sem(f"g_key{b}") for b in range(2)]
        turned, hi_done, lo_done, v_done, v_read = (f.sem(n) for n in ("turned", "hi_done", "lo_done", "v_done", "v_read"))
        s_done, s_read = f.sem("s_done"), f.sem("s_read")
        if attention:
            q = f.sb("q", [P, 2, D])
            prod = f.sb("prod", [P, 2, D])
            ps_q, ps_k, ps_v = f.psum("q", [P, D]), f.psum("k", [P, D]), f.psum("v", [P, D])
            q_done, k_done, q_read, k_read = (f.sem(n) for n in ("q_done", "k_done", "q_read", "k_read"))
        else:
            ps_v, ps_s = f.psum("v", [P, D]), f.psum("s", [P, D])
            w_nat = f.sb("w_nat", [P, KC * D])
            acol = f.sb("acol", [P, 2, KC])
            blocks = f.sb("blocks", [P, 2, KC, H])
            dhi, dlo = f.sb("dhi", [P, 2, KC * H], F32R), f.sb("dlo", [P, 2, KC * H], F32R)
            ps_d = f.psum("d", [P, D])
            d_loaded, blocks_ready, d_done, d_hi, d_lo = (f.sem(n) for n in ("d_loaded", "blocks_ready", "d_done", "d_hi", "d_lo"))

        @f.block.sync
        def _(sp):
            W.load(sp)
            if not attention:
                sp.dma_start(w_nat[:].rearrange("p (k n) -> p k n", n=D),
                             s.inputs[dots[0]].rearrange("(k p) n -> p k n", p=P)).then_inc(d_loaded, 16)
                sp.dma_start(acol[:, 0, :], s.inputs[dots[1]]).then_inc(d_loaded, 16)
                sp.dma_start(acol[:, 1, :], s.inputs[dots[2]]).then_inc(d_loaded, 16)

        @f.block.gpsimd
        def _(pool):
            def step(t):
                r = t.slot(2)
                if t.reuses(2):
                    pool.wait_ge(turned, 2 * (t.m - 1))
                    pool.wait_ge(g_other[r], 16 * t.turn(2))
                    pool.wait_ge(g_key[r], 16 * t.turn(2))
                gather(nc, pool, f.passed_pool, (staged, 2, 1), t, order.other_idx, stage[:, r:r + 1], table, xo[:, r, :], g_other[r])
                gather(nc, pool, f.passed_pool, (staged, 2, 2), t, order.key_idx, stage[:, 2 + r:3 + r], table, xk[:, r, :], g_key[r])
            tiles(pool, ET, 0, step)

        @f.block.vector
        def _(dve):
            W.split_lo(nc, dve)
            if not attention:
                dve.wait_ge(d_loaded, 48)
                for w in range(2):
                    nc.vector.tensor_tensor(blocks[:, w, :, :], s.heads, acol[:, w, :].unsqueeze(2).to_broadcast([P, KC, H]),
                                            ALU.mult).then_inc(blocks_ready, 1)
                dve.wait_ge(d_hi, 1)
                nc.vector.tensor_tensor(dlo[:].rearrange("p w n -> p (w n)"), ps_d[:, 0:2 * KC * H],
                                        dhi[:].rearrange("p w n -> p (w n)").bitcast(F32), ALU.subtract).then_inc(d_lo, 1)

            def step(t):
                if t.exists(ET):
                    b = t.slot(2)
                    for j, w in enumerate("ok"):
                        dve.wait_ge(hi_done, 2 * t.m + 1 + j)
                        nc.vector.tensor_tensor(part[w, "lo"][:, b, :], ps_t[w, b][:], part[w, "hi"][:, b, :].bitcast(F32),
                                                ALU.subtract).then_inc(lo_done, 1)
                t = t.back(1)
                if t.exists(ET):
                    b = t.slot(2)
                    out = scores[:, bass.ts(t.m, H)]
                    if attention:
                        dve.wait_ge(q_read, t.m + 1)
                        dve.wait_ge(k_done, t.m + 1)
                        nc.vector.tensor_tensor(prod[:, b, :], ps_k[:], q[:, b, :], ALU.mult).then_inc(k_read, 1)
                        dve.wait_ge(k_read, t.m + 1)
                        nc.vector.tensor_reduce(out, prod[:, b, :].rearrange("p (h d) -> p h d", d=DH), X, ALU.add).then_inc(s_read, 1)
                    else:
                        dve.wait_ge(s_done, t.m + 1)
                        nc.vector.tensor_copy(out, ps_s[:, 0:H]).then_inc(s_read, 1)
            tiles(dve, ET, 1, step)

        @f.block.scalar
        def _(act):
            W.split_hi(nc, act)
            if not attention:
                act.wait_ge(d_done, 1)
                nc.scalar.activation(dhi[:].rearrange("p w n -> p (w n)"), ps_d[:, 0:2 * KC * H], ACT.Copy).then_inc(d_hi, 1)

            def step(t):
                if t.exists(ET):
                    b = t.slot(2)
                    for j, w in enumerate("ok"):
                        act.wait_ge(turned, 2 * t.m + 1 + j)
                        if t.reuses(2):
                            act.wait_ge(v_done, t.m - 1)
                        nc.scalar.activation(part[w, "hi"][:, b, :], ps_t[w, b][:], ACT.Copy).then_inc(hi_done, 1)
                t = t.back(1)
                if t.exists(ET):
                    b = t.slot(2)
                    if attention:
                        act.wait_ge(q_done, t.m + 1)
                        if t.reuses(2):
                            act.wait_ge(k_read, t.m - 1)
                        nc.scalar.activation(q[:, b, :], ps_q[:], ACT.Copy, scale=DH ** -0.5).then_inc(q_read, 1)
                    act.wait_ge(v_done, t.m + 1)
                    nc.scalar.activation(values[:, bass.ts(t.m, D)], ps_v[:], ACT.Copy).then_inc(v_read, 1)
            tiles(act, ET, 1, step)

        @f.block.tensor
        def _(pe):
            if not attention:
                pe.wait_ge(d_loaded, 48)
                pe.wait_ge(blocks_ready, 2)
                for w in range(2):
                    for m in range(KC):
                        for k in range(KC):
                            mm = pe.matmul(ps_d[:, w * KC * H + m * H:w * KC * H + (m + 1) * H],
                                           w_nat[:, k * D + m * P:k * D + (m + 1) * P], blocks[:, w, k, :],
                                           start=k == 0, stop=k == KC - 1)
                mm.then_inc(d_done, 1)
                pe.wait_ge(d_lo, 1)
            pe.wait_ge(W.lo_done, W.count)

            def step(t):
                if t.exists(ET):
                    b = t.slot(2)
                    for w, x, landed in (("o", xo, g_other), ("k", xk, g_key)):
                        pe.wait_ge(landed[b], 16 * t.turn(2) + 16)
                        if t.reuses(2):
                            pe.wait_ge(lo_done, 2 * (t.m - 1))
                        transpose_tile(pe, ps_t[w, b], x[:, b, :], s.ident).then_inc(turned, 1)
                t = t.back(1)
                if t.exists(ET):
                    b = t.slot(2)
                    hi = {w: part[w, "hi"][:, b, :] for w in "ok"}
                    lo = {w: part[w, "lo"][:, b, :] for w in "ok"}
                    pe.wait_ge(lo_done, 2 * t.m + 2)
                    if attention:
                        if t.reuses(1):
                            pe.wait_ge(q_read, t.m)
                        W.product(pe, ps_q[:], hi["k"], lo["k"], "q").then_inc(q_done, 1)
                        if t.reuses(1):
                            pe.wait_ge(k_read, t.m)
                        W.product(pe, ps_k[:], hi["o"], lo["o"], "k").then_inc(k_done, 1)
                    else:
                        if t.reuses(1):
                            pe.wait_ge(s_read, t.m)
                        n = 0
                        for w, x in ((0, "o"), (1, "k")):
                            for k in range(KC):
                                for xp, wp in ((hi, dhi), (hi, dlo), (lo, dhi)):
                                    mm = pe.matmul(ps_s[:, 0:H], xp[x][:, bass.ts(k, P)], wp[:, w, bass.ts(k, H)],
                                                   start=n == 0, stop=n == 6 * KC - 1)
                                    n += 1
                        mm.then_inc(s_done, 1)
                    if t.reuses(1):
                        pe.wait_ge(v_read, t.m)
                    W.product(pe, ps_v[:], hi["o"], lo["o"], "v").then_inc(v_done, 1)
            tiles(pe, ET, 1, step)


def softmax_weights(nc, s, order, name, scores, gat=False):
    EH = ET * H
    chunks = [(c, min(P, EH - c)) for c in range(0, EH, P)]
    NC = len(chunks)
    with phase(nc, name) as f:
        turned_sb = f.sb("turned_sb", [P, NC, P])
        by_head = f.sb("by_head", [H, SLOTS])
        brk = f.sb("brk", [H, SLOTS])
        fwd = f.sb("fwd", [H, SLOTS])
        back = f.sb("back", [H, SLOTS])
        back_sb = f.sb("back_sb", [P, NC, P])
        ps = [f.psum(f"ps{c}", [P, 512]) for c in range(NC)]
        ps2 = [f.psum(f"ps2{c}", [P, 512]) for c in range(NC)]
        masked, turned, copied, out1, in1 = (f.sem(n) for n in ("masked", "turned", "copied", "out1", "in1"))
        brk_in, back_done, out2, in2, turned2, chain, diff, loads = (f.sem(n) for n in (
            "brk_in", "back_done", "out2", "in2", "turned2", "chain", "diff", "loads"))
        if gat:
            emb = f.sb("emb", [P, NTYPE * H])
            gain = f.sb("gain", [P, EH])
            pick = f.sb("pick", [P, ET])
            term = f.sb("term", [P, EH])

        scratch_in, scratch_back = s.scratch

        @f.block.sync
        def _(sp):
            sp.dma_start(brk[:], order.breaks.rearrange("t p -> (t p)").partition_broadcast(H)).then_inc(brk_in, 16)
            if gat:
                sp.dma_start(emb[:], s.inputs["et_emb"].partition_broadcast(P)).then_inc(loads, 16)
            sp.wait_ge(copied, NC)
            for c, (lo, w) in enumerate(chunks):
                sp.dma_start(scratch_in[lo:lo + w, :], turned_sb[0:w, c, :]).then_inc(out1, 16)
            sp.wait_ge(out1, 16 * NC)
            sp.dma_start(by_head[:].rearrange("h (t s) -> h t s", s=P),
                         scratch_in.rearrange("(t h) s -> h t s", h=H)).then_inc(in1, 16)
            sp.wait_ge(back_done, 2)
            sp.dma_start(scratch_back.rearrange("(t h) s -> h t s", h=H),
                         back[:].rearrange("h (t s) -> h t s", s=P)).then_inc(out2, 16)
            sp.wait_ge(out2, 16)
            for c, (lo, w) in enumerate(chunks):
                sp.dma_start(back_sb[0:w, c, :], scratch_back[lo:lo + w, :]).then_inc(in2, 16)

        @f.block.vector
        def _(dve):
            n = [0]

            def link(ins):
                n[0] += 1
                ins.then_inc(chain, 1)
                dve.wait_ge(chain, n[0])

            sc = scores[:]
            if gat:
                link(nc.vector.tensor_scalar(term[:], sc, 0.2, None, ALU.mult))
                link(nc.vector.tensor_tensor(sc, sc, term[:], ALU.max))
                dve.wait_ge(loads, 16)
                link(nc.vector.memset(gain[:], 1.0))
                cube = [P, ET, H]
                v3 = lambda a: a.rearrange("p (t h) -> p t h", h=H)
                for k in range(NTYPE):
                    link(nc.vector.tensor_scalar(pick[:], order.type_col[:], float(k), None, ALU.is_equal))
                    link(nc.vector.tensor_tensor(v3(term[:]), pick[:].unsqueeze(2).to_broadcast(cube),
                                                 emb[:, bass.ts(k, H)].unsqueeze(1).to_broadcast(cube), ALU.mult))
                    link(nc.vector.tensor_tensor(gain[:], gain[:], term[:], ALU.add))
                link(nc.vector.tensor_tensor(sc, sc, gain[:], ALU.mult))
                link(nc.vector.tensor_tensor(v3(sc), v3(sc), order.weight_col[:].unsqueeze(2).to_broadcast(cube), ALU.mult))
            nc.vector.memset(scores[0:1, :], FAR).then_inc(masked, 1)
            for c, (lo, w) in enumerate(chunks):
                dve.wait_ge(turned, c + 1)
                nc.vector.tensor_copy(turned_sb[0:w, c, :], ps[c][0:w, 0:P]).then_inc(copied, 1)
            dve.wait_ge(in1, 16)
            dve.wait_ge(brk_in, 16)
            link(nc.vector.tensor_tensor_scan(fwd[:], brk[:], by_head[:], FAR, ALU.add, ALU.max))
            nc.vector.tensor_tensor_scan(back[:, 0:SLOTS - 1][:, ::-1], brk[:, 1:SLOTS][:, ::-1], fwd[:, 0:SLOTS - 1][:, ::-1],
                                         fwd[:, SLOTS - 1:SLOTS], ALU.add, ALU.max).then_inc(back_done, 1)
            nc.vector.tensor_copy(back[:, SLOTS - 1:SLOTS], fwd[:, SLOTS - 1:SLOTS]).then_inc(back_done, 1)
            dve.wait_ge(turned2, NC)
            for c, (lo, w) in enumerate(chunks):
                part = scores[:, lo:lo + w]
                if gat:
                    link(nc.vector.tensor_scalar(term[:, lo:lo + w], ps2[c][:, 0:w], 0.0, None, ALU.max))
                    top = term[:, lo:lo + w]
                else:
                    top = ps2[c][:, 0:w]
                nc.vector.tensor_tensor(part, part, top, ALU.subtract).then_inc(diff, 1)

        @f.block.tensor
        def _(pe):
            pe.wait_ge(masked, 1)
            for c, (lo, w) in enumerate(chunks):
                pe.transpose(ps[c][0:w, 0:P], scores[:, lo:lo + w], s.ident).then_inc(turned, 1)
            pe.wait_ge(in2, 16 * NC)
            for c, (lo, w) in enumerate(chunks):
                pe.transpose(ps2[c][:, 0:w], back_sb[0:w, c, :], s.ident[0:w, 0:w]).then_inc(turned2, 1)

        @f.block.scalar
        def _(act):
            act.wait_ge(diff, NC)
            nc.scalar.activation(scores[:], scores[:], ACT.Exp)



def node_sage(nc, s, order):
    with phase(nc, "sage") as f:
        x, u, g = f.sb("x", [P, 4, D]), f.sb("u", [P, 4, D]), f.sb("g", [P, 4, D])
        t_sum, r, y, z = (f.sb(n, [P, 2, D]) for n in ("t_sum", "r", "y", "z"))
        stats, mv, dev, rstd = f.sb("stats", [P, 2, 6]), f.sb("mv", [P, 2, 2]), f.sb("dev", [P, 2, 1]), f.sb("rstd", [P, 2, 1])
        dev_done = f.sem("dev_done")
        stage = f.sb("stage", [P, 4], I32)
        loaded = [f.sem(f"loaded{b}") for b in range(4)]
        gathered = [f.sem(f"gathered{b}") for b in range(4)]
        stored = [f.sem(f"stored{b}") for b in range(2)]
        staged, summed, rect, steps_s = f.sem("staged"), f.sem("summed"), f.sem("rect"), f.sem("steps")

        @f.block.sync
        def _(sp):
            def step(t):
                if t.exists(NT):
                    r4 = t.slot(4)
                    if t.reuses(4):
                        sp.wait_ge(steps_s, 5 * (t.m - 3))
                    sp.dma_start(x[:, r4, :], rows(s.inputs["x"], t.m)).then_inc(loaded[r4], 16)
                    sp.dma_start(u[:, r4, :], rows(s.root, t.m)).then_inc(loaded[r4], 16)
                t = t.back(3)
                if t.exists(NT):
                    sp.wait_ge(steps_s, 5 * t.m + 5)
                    sp.dma_start(rows(s.x1, t.m), z[:, t.slot(2), :]).then_inc(stored[t.slot(2)], 16)
            tiles(sp, NT, 3, step)
            for b in range(2):
                sp.wait_ge(stored[b], 16 * (NT // 2))

        @f.block.gpsimd
        def _(pool):
            def step(t):
                r4 = t.slot(4)
                if t.reuses(4):
                    pool.wait_ge(summed, t.m - 3)
                    pool.wait_ge(gathered[r4], 16 * t.turn(4))
                gather(nc, pool, f.passed_pool, (staged, 1, 1), t, order.place, stage[:, r4:r4 + 1], s.edge_out, g[:, r4, :], gathered[r4])
            tiles(pool, NT, 0, step)

        @f.block.vector
        def _(dve):
            steps = Steps(dve, steps_s, 5)

            def step(t):
                now, before = t, t.back(1)
                if before.exists(NT):
                    b, r4 = before.slot(2), before.slot(4)
                    st = steps.tile(before.m)
                    dve.wait_ge(rect, before.m + 1)
                    st(nc.vector.scalar_tensor_tensor(y[:, b, :], x[:, r4, :], 2.0, r[:, b, :], ALU.mult, ALU.add))
                    norm_stats(nc, st, f.passed_dve, stats[:, b, :], mv[:, b, :], y[:, b, :])
                if now.exists(NT):
                    b, r4 = now.slot(2), now.slot(4)
                    dve.wait_ge(loaded[r4], 32 * now.turn(4) + 32)
                    dve.wait_ge(gathered[r4], 16 * now.turn(4) + 16)
                    if now.reuses(2):
                        dve.wait_ge(rect, now.m - 1)
                    nc.vector.tensor_tensor(t_sum[:, b, :], u[:, r4, :], g[:, r4, :], ALU.add).then_inc(summed, 1)
                if before.exists(NT):
                    b = before.slot(2)
                    dve.wait_ge(dev_done, before.m + 1)
                    st(nc.vector.reciprocal(rstd[:, b, :], dev[:, b, :]))
                    if before.reuses(2):
                        dve.wait_ge(stored[b], 16 * before.turn(2))
                    st.last(nc.vector.tensor_scalar(z[:, b, :], y[:, b, :], mv[:, b, 0:1], rstd[:, b, :], ALU.subtract, ALU.mult))
            tiles(dve, NT, 1, step)

        @f.block.scalar
        def _(act):
            nc.scalar.preload_act_table(ACT.Sqrt)

            def step(t):
                now, before = t, t.back(1)
                if before.exists(NT):
                    b = before.slot(2)
                    act.wait_ge(steps_s, 5 * before.m + 3)
                    deviation(nc, s, dev[:, b, :], mv[:, b, :]).then_inc(dev_done, 1)
                if now.exists(NT):
                    b = now.slot(2)
                    act.wait_ge(summed, now.m + 1)
                    if now.reuses(2):
                        act.wait_ge(steps_s, 5 * (now.m - 1))
                    nc.scalar.activation(r[:, b, :], t_sum[:, b, :], ACT.Relu).then_inc(rect, 1)
            tiles(act, NT, 1, step)


def node_ffn(nc, s, order):
    with phase(nc, "ffn") as f:
        x, g = f.sb("x", [P, 4, D]), f.sb("g", [P, 4, D])
        y = f.sb("y", [P, 2, D])
        z1 = f.sb("z1", [P, 2, D])
        res = f.sb("res", [P, 4, D])
        y2 = f.sb("y2", [P, 2, D])
        z2 = f.sb("z2", [P, 2, D])
        y3, z3 = f.sb("y3", [P, 2, D]), f.sb("z3", [P, 2, D])
        stats, mv, dev, rstd = f.sb("stats", [P, 6, 6]), f.sb("mv", [P, 6, 2]), f.sb("dev", [P, 6, 1]), f.sb("rstd", [P, 6, 2])
        dev1, dev2, dev3 = f.sem("dev1"), f.sem("dev2"), f.sem("dev3")
        stage = f.sb("stage", [P, 4], I32)
        hi, lo = f.sb("hi", [P, 2, D], F32R), f.sb("lo", [P, 2, D], F32R)
        hid, hid_hi, hid_lo = f.sb("hid", [DFF, 2, P]), f.sb("hid_hi", [DFF, 2, P], F32R), f.sb("hid_lo", [DFF, 2, P], F32R)
        rows_in = f.sb("rows_in", [P, 5, D])
        shift = f.sb("shift", [P, D])
        gcol, bcol, b1 = f.sb("gcol", [P, KC]), f.sb("bcol", [P, KC]), f.sb("b1", [DFF, 1])
        bias1 = f.sb("bias1", [DFF, 1])
        w1p = f.sb("w1p", [P, KC * DFF])
        w2 = f.sb("w2", [DFF, D])
        w2_hi, w2_lo = f.sb("w2_hi", [DFF, D], F32R), f.sb("w2_lo", [DFF, D], F32R)
        W = Weights(f, {"w1": (s.inputs["w1"], DFF)}, {"w1": gcol})
        ps_t = [f.psum(f"t{b}", [P, D]) for b in range(2)]
        ps_h = [f.psum(f"h{b}", [P, D]) for b in range(2)]
        ps_f = [f.psum(f"f{b}", [P, D]) for b in range(2)]
        params, shift_ready, w2h, w2l, bias_made, bias_ready = (f.sem(n) for n in (
            "params", "shift_ready", "w2h", "w2l", "bias_made", "bias_ready"))
        loaded = [f.sem(f"loaded{b}") for b in range(4)]
        gathered = [f.sem(f"gathered{b}") for b in range(4)]
        stored = [f.sem(f"stored{b}") for b in range(2)]
        staged, s1, z1_done, gained, turned, hi_done, lo_done, h_done, relu_done, hh, hl, f_done = (f.sem(n) for n in (
            "staged", "s1", "z1_done", "gained", "turned", "hi_done", "lo_done", "h_done", "relu_done", "hh", "hl", "f_done"))
        s2, z2_done, s3, z3_done = (f.sem(n) for n in ("s2", "z2_done", "s3", "z3_done"))
        res_done = f.sem("res_done")
        y3_gain, y3_shift = f.sem("y3_gain"), f.sem("y3_shift")

        @f.block.sync
        def _(sp):
            for ap, src in ((gcol[:], s.inputs["ln1_g_col"]), (bcol[:], s.inputs["ln1_b_col"]), (b1[:], s.inputs["b1_col"]),
                            (w1p[:].rearrange("p (k n) -> p k n", n=DFF), s.inputs["w1"].rearrange("(k p) n -> p k n", p=P)), (w2[:], s.inputs["w2"])):
                sp.dma_start(ap, src).then_inc(params, 16)
            for j, src in enumerate((s.inputs["ln1_g"], s.inputs["ln1_b"], s.inputs["b2"], s.inputs["ln2_g"], s.inputs["ln2_b"])):
                sp.dma_start(rows_in[:, j, :], src.partition_broadcast(P)).then_inc(params, 16)
            W.load(sp)

            def step(t):
                if t.exists(NT):
                    r4 = t.slot(4)
                    if t.reuses(4):
                        sp.wait_ge(s3, 5 * (t.m - 3))
                    sp.dma_start(x[:, r4, :], rows(s.x1, t.m)).then_inc(loaded[r4], 16)
                t = t.back(4)
                if t.exists(NT):
                    sp.wait_ge(z3_done, t.m + 1)
                    sp.dma_start(rows(s.x2, t.m), z3[:, t.slot(2), :]).then_inc(stored[t.slot(2)], 16)
            tiles(sp, NT, 4, step)
            for b in range(2):
                sp.wait_ge(stored[b], 16 * (NT // 2))

        @f.block.gpsimd
        def _(pool):
            pool.wait_ge(params, 160)
            nc.gpsimd.tensor_tensor(shift[:], rows_in[:, 1, :], rows_in[:, 2, :], ALU.add).then_inc(shift_ready, 1)
            pool.wait_ge(shift_ready, 1)

            def step(t):
                if t.exists(NT):
                    r4 = t.slot(4)
                    if t.reuses(4):
                        pool.wait_ge(s1, 5 * (t.m - 3))
                        pool.wait_ge(gathered[r4], 16 * t.turn(4))
                    gather(nc, pool, f.passed_pool, (staged, 1, 1), t, order.place, stage[:, r4:r4 + 1], s.edge_out, g[:, r4, :], gathered[r4])
                t = t.back(1)
                if t.exists(NT):
                    b, r4 = t.slot(2), t.slot(4)
                    pool.wait_ge(z1_done, t.m + 1)
                    if t.reuses(4):
                        pool.wait_ge(s2, 5 * (t.m - 3))
                    nc.gpsimd.tensor_tensor(res[:, r4, :], z1[:, b, :], rows_in[:, 0, :], ALU.mult).then_inc(gained, 1)
                    pool.wait_ge(gained, t.m + 1)
                    nc.gpsimd.tensor_tensor(res[:, r4, :], res[:, r4, :], shift[:], ALU.add).then_inc(res_done, 1)
            tiles(pool, NT, 1, step)

        @f.block.vector
        def _(dve):
            st1, st2, st3 = Steps(dve, s1, 5), Steps(dve, s2, 5), Steps(dve, s3, 5)
            W.split_lo(nc, dve)
            dve.wait_ge(w2h, 1)
            nc.vector.tensor_tensor(w2_lo[:], w2[:], w2_hi[:].bitcast(F32), ALU.subtract).then_inc(w2l, 1)
            dve.wait_ge(bias_made, 1)
            nc.vector.tensor_tensor(bias1[:], b1[:], ps_h[0][0:DFF, 0:1], ALU.add).then_inc(bias_ready, 1)

            def stats_of(st, j, src):
                norm_stats(nc, st, f.passed_dve, stats[:, j, :], mv[:, j, :], src)

            def scale_of(st, j, done, t):
                dve.wait_ge(done, t.m + 1)
                norm_scale(nc, st, mv[:, j, :], dev[:, j, :], rstd[:, j, :])

            def step(t):
                t0, t1, t2, t3 = t, t.back(1), t.back(2), t.back(3)
                b0, b1, b2, b3 = t0.slot(2), t1.slot(2), t2.slot(2), t3.slot(2)
                if t0.exists(NT):
                    r4 = t0.slot(4)
                    st1.tile(t0.m)
                    dve.wait_ge(loaded[r4], 16 * t0.turn(4) + 16)
                    dve.wait_ge(gathered[r4], 16 * t0.turn(4) + 16)
                    if t0.reuses(2):
                        dve.wait_ge(z1_done, t0.m - 1)
                    st1(nc.vector.tensor_tensor(y[:, b0, :], x[:, r4, :], g[:, r4, :], ALU.add))
                    stats_of(st1, b0, y[:, b0, :])
                if t1.exists(NT):
                    dve.wait_ge(hi_done, t1.m + 1)
                    nc.vector.tensor_tensor(lo[:, b1, :], ps_t[b1][:], hi[:, b1, :].bitcast(F32), ALU.subtract).then_inc(lo_done, 1)
                if t0.exists(NT):
                    scale_of(st1, b0, dev1, t0)
                if t1.exists(NT):
                    dve.wait_ge(hh, t1.m + 1)
                    nc.vector.tensor_tensor(hid_lo[:, b1, :], hid[:, b1, :], hid_hi[:, b1, :].bitcast(F32), ALU.subtract).then_inc(hl, 1)
                if t2.exists(NT):
                    st2.tile(t2.m)
                    dve.wait_ge(f_done, t2.m + 1)
                    dve.wait_ge(res_done, t2.m + 1)
                    if t2.reuses(2):
                        dve.wait_ge(z2_done, t2.m - 1)
                    st2(nc.vector.tensor_tensor(y2[:, b2, :], ps_f[b2][:], res[:, t2.slot(4), :], ALU.add))
                    stats_of(st2, 2 + b2, y2[:, b2, :])
                if t3.exists(NT):
                    st3.tile(t3.m)
                    dve.wait_ge(z2_done, t3.m + 1)
                    if t3.reuses(2):
                        dve.wait_ge(z3_done, t3.m - 1)
                    nc.vector.tensor_tensor(y3[:, b3, :], z2[:, b3, :], rows_in[:, 3, :], ALU.mult).then_inc(y3_gain, 1)
                    dve.wait_ge(y3_gain, t3.m + 1)
                    nc.vector.tensor_tensor(y3[:, b3, :], y3[:, b3, :], rows_in[:, 4, :], ALU.add).then_inc(y3_shift, 1)
                    dve.wait_ge(y3_shift, t3.m + 1)
                    st3(nc.vector.tensor_tensor(y3[:, b3, :], y3[:, b3, :], x[:, t3.slot(4), :], ALU.add))
                    stats_of(st3, 4 + b3, y3[:, b3, :])
                if t2.exists(NT):
                    scale_of(st2, 2 + b2, dev2, t2)
                if t3.exists(NT):
                    scale_of(st3, 4 + b3, dev3, t3)
            tiles(dve, NT, 3, step)


        @f.block.scalar
        def _(act):
            nc.scalar.preload_act_table(ACT.Sqrt)
            W.split_hi(nc, act)
            act.wait_ge(params, 160)
            nc.scalar.activation(w2_hi[:], w2[:], ACT.Copy).then_inc(w2h, 1)
            act.wait_ge(bias_ready, 1)

            def step(t):
                if t.exists(NT):
                    b = t.slot(2)
                    act.wait_ge(s1, 5 * t.m + 3)
                    deviation(nc, s, dev[:, b, :], mv[:, b, :]).then_inc(dev1, 1)
                    act.wait_ge(s1, 5 * t.m + 5)
                    if t.reuses(2):
                        act.wait_ge(turned, t.m - 1)
                        act.wait_ge(res_done, t.m - 1)
                    nc.scalar.activation(z1[:, b, :], y[:, b, :], ACT.Identity, bias=rstd[:, b, 1:2], scale=rstd[:, b, 0:1]).then_inc(z1_done, 1)
                    act.wait_ge(turned, t.m + 1)
                    if t.reuses(2):
                        act.wait_ge(h_done, t.m - 1)
                    nc.scalar.activation(hi[:, b, :], ps_t[b][:], ACT.Copy).then_inc(hi_done, 1)
                t = t.back(1)
                if t.exists(NT):
                    b = t.slot(2)
                    act.wait_ge(h_done, t.m + 1)
                    if t.reuses(2):
                        act.wait_ge(hl, t.m - 1)
                        act.wait_ge(f_done, t.m - 1)
                    nc.scalar.activation(hid[:, b, :], ps_h[b][0:DFF, 0:P], ACT.Relu, bias=bias1[:]).then_inc(relu_done, 1)
                    act.wait_ge(relu_done, t.m + 1)
                    nc.scalar.activation(hid_hi[:, b, :], hid[:, b, :], ACT.Copy).then_inc(hh, 1)
                t = t.back(1)
                if t.exists(NT):
                    b = t.slot(2)
                    act.wait_ge(s2, 5 * t.m + 3)
                    deviation(nc, s, dev[:, 2 + b, :], mv[:, 2 + b, :]).then_inc(dev2, 1)
                    act.wait_ge(s2, 5 * t.m + 5)
                    if t.reuses(2):
                        act.wait_ge(y3_gain, t.m - 1)
                    nc.scalar.activation(z2[:, b, :], y2[:, b, :], ACT.Identity, bias=rstd[:, 2 + b, 1:2], scale=rstd[:, 2 + b, 0:1]).then_inc(z2_done, 1)
                t = t.back(1)
                if t.exists(NT):
                    b = t.slot(2)
                    act.wait_ge(s3, 5 * t.m + 3)
                    deviation(nc, s, dev[:, 4 + b, :], mv[:, 4 + b, :]).then_inc(dev3, 1)
                    act.wait_ge(s3, 5 * t.m + 5)
                    if t.reuses(2):
                        act.wait_ge(stored[b], 16 * t.turn(2))
                    nc.scalar.activation(z3[:, b, :], y3[:, b, :], ACT.Identity, bias=rstd[:, 4 + b, 1:2], scale=rstd[:, 4 + b, 0:1]).then_inc(z3_done, 1)
            tiles(act, NT, 3, step)

        @f.block.tensor
        def _(pe):
            pe.wait_ge(params, 160)
            for k in range(KC):
                mm = pe.matmul(ps_h[0][0:DFF, 0:1], w1p[:, bass.ts(k, DFF)], bcol[:, k:k + 1], start=k == 0, stop=k == KC - 1)
            mm.then_inc(bias_made, 1)
            pe.wait_ge(W.lo_done, 1)
            pe.wait_ge(w2l, 1)
            pe.wait_ge(bias_ready, 1)

            def step(t):
                if t.exists(NT):
                    b = t.slot(2)
                    pe.wait_ge(z1_done, t.m + 1)
                    if t.reuses(2):
                        pe.wait_ge(lo_done, t.m - 1)
                    transpose_tile(pe, ps_t[b], z1[:, b, :], s.ident).then_inc(turned, 1)
                t = t.back(1)
                if t.exists(NT):
                    b = t.slot(2)
                    pe.wait_ge(lo_done, t.m + 1)
                    if t.reuses(2):
                        pe.wait_ge(relu_done, t.m - 1)
                    n = 0
                    for k in range(KC):
                        for wp, xp in ((W.hi, hi), (W.hi, lo), (W.lo, hi)):
                            mm = pe.matmul(ps_h[b][0:DFF, 0:P], wp["w1"][:, bass.ts(k, DFF)], xp[:, b, bass.ts(k, P)],
                                           start=n == 0, stop=n == 3 * KC - 1)
                            n += 1
                    mm.then_inc(h_done, 1)
                t = t.back(0)
                if t.exists(NT):
                    b = t.slot(2)
                    pe.wait_ge(hl, t.m + 1)
                    if t.reuses(2):
                        pe.wait_ge(s2, 5 * (t.m - 1))
                    for n, (xp, wp) in enumerate(((hid_hi, w2_hi), (hid_hi, w2_lo), (hid_lo, w2_hi))):
                        mm = pe.matmul(ps_f[b][:], xp[:, b, :], wp[:], start=n == 0, stop=n == 2)
                    mm.then_inc(f_done, 1)
            tiles(pe, NT, 1, step)


def node_residual(nc, s, order, name, x_in, x_out, affine=None):
    with phase(nc, name) as f:
        x, g = f.sb("x", [P, 4, D]), f.sb("g", [P, 4, D])
        y, y2, z = f.sb("y", [P, 2, D]), f.sb("y2", [P, 2, D]), f.sb("z", [P, 2, D])
        stats, mv, dev, rstd = f.sb("stats", [P, 4, 6]), f.sb("mv", [P, 4, 2]), f.sb("dev", [P, 4, 1]), f.sb("rstd", [P, 4, 2])
        dev1, dev2 = f.sem("dev1"), f.sem("dev2")
        stage = f.sb("stage", [P, 4], I32)
        loaded = [f.sem(f"loaded{b}") for b in range(4)]
        gathered = [f.sem(f"gathered{b}") for b in range(4)]
        stored = [f.sem(f"stored{b}") for b in range(2)]
        staged, s1, s2, z_done = f.sem("staged"), f.sem("s1"), f.sem("s2"), f.sem("z_done")
        if affine:
            z1 = f.sb("z1", [P, 2, D])
            aff = f.sb("aff", [P, 2, D])
            params, z1_done, gained, shifted = (f.sem(n) for n in ("params", "z1_done", "gained", "shifted"))
        final, FS = (s2, 5) if affine else (s1, 5)

        @f.block.sync
        def _(sp):
            if affine:
                for j in range(2):
                    sp.dma_start(aff[:, j, :], affine[j].partition_broadcast(P)).then_inc(params, 16)

            def step(t):
                if t.exists(NT):
                    r4 = t.slot(4)
                    if t.reuses(4):
                        sp.wait_ge(final, FS * (t.m - 3))
                    sp.dma_start(x[:, r4, :], rows(x_in, t.m)).then_inc(loaded[r4], 16)
                t = t.back(3)
                if t.exists(NT):
                    sp.wait_ge(z_done, t.m + 1)
                    sp.dma_start(rows(x_out, t.m), z[:, t.slot(2), :]).then_inc(stored[t.slot(2)], 16)
            tiles(sp, NT, 3, step)
            for b in range(2):
                sp.wait_ge(stored[b], 16 * (NT // 2))

        @f.block.gpsimd
        def _(pool):
            if affine:
                pool.wait_ge(params, 32)

            def step(t):
                if t.exists(NT):
                    r4 = t.slot(4)
                    if t.reuses(4):
                        pool.wait_ge(s1, 5 * (t.m - 3))
                        pool.wait_ge(gathered[r4], 16 * t.turn(4))
                    gather(nc, pool, f.passed_pool, (staged, 1, 1), t, order.place, stage[:, r4:r4 + 1], s.edge_out, g[:, r4, :], gathered[r4])
                if not affine:
                    return
                t = t.back(1)
                if t.exists(NT):
                    b = t.slot(2)
                    pool.wait_ge(z1_done, t.m + 1)
                    nc.gpsimd.tensor_tensor(z1[:, b, :], z1[:, b, :], aff[:, 0, :], ALU.mult).then_inc(gained, 1)
            tiles(pool, NT, 1 if affine else 0, step)

        @f.block.vector
        def _(dve):
            st1, st2 = Steps(dve, s1, 5), Steps(dve, s2, 5)
            if affine:
                dve.wait_ge(params, 32)

            def stats_of(st, j, src):
                norm_stats(nc, st, f.passed_dve, stats[:, j, :], mv[:, j, :], src)

            def scale_of(st, j, done, t):
                dve.wait_ge(done, t.m + 1)
                norm_scale(nc, st, mv[:, j, :], dev[:, j, :], rstd[:, j, :])

            def step(t):
                t2 = t.back(2)
                b, b2 = t.slot(2), t2.slot(2)
                if t.exists(NT):
                    r4 = t.slot(4)
                    st1.tile(t.m)
                    dve.wait_ge(loaded[r4], 16 * t.turn(4) + 16)
                    dve.wait_ge(gathered[r4], 16 * t.turn(4) + 16)
                    if t.reuses(2):
                        dve.wait_ge(z1_done if affine else z_done, t.m - 1)
                    st1(nc.vector.tensor_tensor(y[:, b, :], x[:, r4, :], g[:, r4, :], ALU.add))
                    stats_of(st1, b, y[:, b, :])
                if affine and t2.exists(NT):
                    st2.tile(t2.m)
                    dve.wait_ge(gained, t2.m + 1)
                    if t2.reuses(2):
                        dve.wait_ge(z_done, t2.m - 1)
                    nc.vector.tensor_tensor(y2[:, b2, :], z1[:, b2, :], aff[:, 1, :], ALU.add).then_inc(shifted, 1)
                    dve.wait_ge(shifted, t2.m + 1)
                    st2(nc.vector.tensor_tensor(y2[:, b2, :], y2[:, b2, :], x[:, t2.slot(4), :], ALU.add))
                    stats_of(st2, 2 + b2, y2[:, b2, :])
                if t.exists(NT):
                    scale_of(st1, b, dev1, t)
                if affine and t2.exists(NT):
                    scale_of(st2, 2 + b2, dev2, t2)
            tiles(dve, NT, 2 if affine else 0, step)

        @f.block.scalar
        def _(act):
            nc.scalar.preload_act_table(ACT.Sqrt)

            def step(t):
                t2 = t.back(2)
                b, b2 = t.slot(2), t2.slot(2)
                if t.exists(NT):
                    act.wait_ge(s1, 5 * t.m + 3)
                    deviation(nc, s, dev[:, b, :], mv[:, b, :]).then_inc(dev1, 1)
                if affine and t2.exists(NT):
                    act.wait_ge(s2, 5 * t2.m + 3)
                    deviation(nc, s, dev[:, 2 + b2, :], mv[:, 2 + b2, :]).then_inc(dev2, 1)
                if affine and t.exists(NT):
                    act.wait_ge(s1, 5 * t.m + 5)
                    if t.reuses(2):
                        act.wait_ge(shifted, t.m - 1)
                    nc.scalar.activation(z1[:, b, :], y[:, b, :], ACT.Identity, bias=rstd[:, b, 1:2], scale=rstd[:, b, 0:1]).then_inc(z1_done, 1)
                t = t2 if affine else t
                if t.exists(NT):
                    b = t.slot(2)
                    src, j, sem = (y2, 2 + b, s2) if affine else (y, b, s1)
                    act.wait_ge(sem, 5 * t.m + 5)
                    if t.reuses(2):
                        act.wait_ge(stored[b], 16 * t.turn(2))
                    nc.scalar.activation(z[:, b, :], src[:, b, :], ACT.Identity, bias=rstd[:, j, 1:2], scale=rstd[:, j, 0:1]).then_inc(z_done, 1)
            tiles(act, NT, 2 if affine else 0, step)



def gnn_program(nc, a, out):
    with ExitStack() as ctx:
        def sb(n, shape, dt=F32):
            return ctx.enter_context(nc.sbuf_tensor(n, shape, dt))

        def dram(n, shape, dt=F32):
            return nc.dram_tensor(n, shape, dt, kind="Internal").ap()

        s = Names()
        s.inputs = a
        s.packed = sb("packed", [P, CW])
        s.root, s.x1, s.x2, s.x3 = (dram(n, [NP, D]) for n in ("root_d", "x1_d", "x2_d", "x3_d"))
        s.edge_out = dram("edge_out_d", [SLOTS + P, D])
        s.scratch = [dram(f"scratch{i}_d", [ET * H, P]) for i in range(2)]
        s.iota, s.ident, s.earlier, s.above, s.ones, s.zrow = (s.packed[:, j * P:(j + 1) * P] for j in range(len(CONSTS)))
        c = len(CONSTS) * P
        s.heads = s.packed[:, c:c + KC * H].rearrange("p (k h) -> p k h", h=H)
        s.part = s.packed[:, c + KC * H:c + KC * H + 1]
        s.eps = s.packed[:, c + KC * H + 1:c + KC * H + 2]

        def order(key):
            o = Names()
            o.key = key
            o.table = dram(f"table{key}_d", [SLOTS, 4])
            o.key_out = dram(f"key_out{key}_d", [SLOTS])
            o.key_in = dram(f"key_in{key}_d", [ET, P])
            o.breaks = dram(f"breaks{key}_d", [ET, P])
            o.key_in_col = sb(f"key_in_col{key}", [P, ET])
            o.other_idx, o.key_idx = sb(f"other_idx{key}", [P, ET], I32), sb(f"key_idx{key}", [P, ET], I32)
            o.type_col, o.weight_col = sb(f"type_col{key}", [P, ET]), sb(f"weight_col{key}", [P, ET])
            o.place = sb(f"place{key}", [P, NT], I32)
            return o

        by_dst, by_src = order(DST), order(SRC)
        load_constants(nc, s)
        sort_edges(nc, s, by_dst)
        sort_edges(nc, s, by_src)

        dense_root(nc, s)
        aggregate(nc, s, by_dst, "agg0", source=s.inputs["x"], matrix=s.inputs["wl_t"])
        node_sage(nc, s, by_dst)

        with nc.sbuf_tensor("values", [P, ET * D], F32) as values, nc.sbuf_tensor("scores", [P, ET * H], F32) as scores:
            edge_products(nc, s, by_dst, "qkv1", s.x1, {"k": (s.inputs["wk"], D), "v": (s.inputs["wv"], D)}, {"q": (s.inputs["wq"], D)}, values, scores)
            softmax_weights(nc, s, by_dst, "soft1", scores)
            aggregate(nc, s, by_dst, "agg1", values=values, weights=scores, matrix=s.inputs["wo"])
        node_ffn(nc, s, by_dst)

        with nc.sbuf_tensor("values2", [P, ET * D], F32) as values, nc.sbuf_tensor("scores2", [P, ET * H], F32) as scores:
            edge_products(nc, s, by_dst, "gat2", s.x2, {"v": (s.inputs["w_gat_t"], D)}, {}, values, scores,
                          dots=("w_gat", "a_src_col", "a_dst_col"))
            softmax_weights(nc, s, by_dst, "soft2", scores, gat=True)
            aggregate(nc, s, by_dst, "agg2", values=values, weights=scores, small=1e-10)
        node_residual(nc, s, by_dst, "res2", s.x2, s.x3, affine=(s.inputs["gat_g"], s.inputs["gat_b"]))

        with nc.sbuf_tensor("values3", [P, ET * D], F32) as values, nc.sbuf_tensor("scores3", [P, ET * H], F32) as scores:
            edge_products(nc, s, by_src, "qkv3", s.x3, {"k": (s.inputs["w3"][:, D:2 * D], D), "v": (s.inputs["w3"][:, 2 * D:3 * D], D)},
                          {"q": (s.inputs["w3"][:, 0:D], D)}, values, scores)
            softmax_weights(nc, s, by_src, "soft3", scores)
            aggregate(nc, s, by_src, "agg3", values=values, weights=scores)
        node_residual(nc, s, by_src, "res3", s.x3, out)


def kernel(**inputs):
    import concourse.bacc as bacc
    from concourse.bass_utils import run_bass_kernel_spmd

    v = {k: np.asarray(a) for k, a in inputs.items()}
    flip = lambda m: np.ascontiguousarray(m.T)
    col = lambda m: np.ascontiguousarray(m.reshape(-1, P).T)
    edge_col = lambda m: np.ascontiguousarray(m.reshape(ET, EC).T)
    packed, table = host_constants()
    x = np.zeros((NP, D), v["x"].dtype)
    x[:N] = v["x"]
    arrays = {
        "x": x, "consts_dram": packed, "table_default": table,
        "src_flat": v["src"], "dst_flat": v["dst"], "src_col": edge_col(v["src"]), "dst_col": edge_col(v["dst"]),
        "type_col": edge_col(v["edge_type_8"]), "weight_col": edge_col(v["edge_weight"]),
        "ln0_g_col": col(v["L0_gnn_ln_gamma"]), "ln0_b_col": col(v["L0_gnn_ln_beta"]),
        "wl_t": flip(v["L0_gnn_w_l"]), "wr_t": flip(v["L0_gnn_w_r"]), "b_l": v["L0_gnn_b_l"],
        "wq": v["L1_gnn_Wq"], "wk": v["L1_gnn_Wk"], "wv": v["L1_gnn_Wv"], "wo": v["L1_gnn_Wo"],
        "ln1_g": v["L1_gnn_ln1_g"], "ln1_b": v["L1_gnn_ln1_b"], "ln2_g": v["L1_gnn_ln2_g"], "ln2_b": v["L1_gnn_ln2_b"],
        "ln1_g_col": col(v["L1_gnn_ln1_g"]), "ln1_b_col": col(v["L1_gnn_ln1_b"]),
        "w1": v["L1_gnn_W1"], "b1_col": v["L1_gnn_b1"].reshape(DFF, 1), "w2": v["L1_gnn_W2"], "b2": v["L1_gnn_b2"],
        "w_gat": v["L2_gnn_W"], "w_gat_t": flip(v["L2_gnn_W"]),
        "a_src_col": col(v["L2_gnn_a_src"].reshape(-1)), "a_dst_col": col(v["L2_gnn_a_dst"].reshape(-1)),
        "et_emb": v["L2_gnn_et_emb"].reshape(-1), "gat_g": v["L2_gnn_ln_gamma"], "gat_b": v["L2_gnn_ln_beta"],
        "w3": v["L3_gnn_W"],
    }
    arrays = {k: np.ascontiguousarray(m) for k, m in arrays.items()}
    nc = bacc.Bacc("TRN2", target_bir_lowering=False, num_devices=1)
    aps = {k: nc.dram_tensor(f"in_{k}", m.shape, mybir.dt.from_np(m.dtype), kind="ExternalInput").ap() for k, m in arrays.items()}
    out = nc.dram_tensor("out", [NP, D], F32, kind="ExternalOutput").ap()
    gnn_program(nc, aps, out)
    r = run_bass_kernel_spmd(nc, [{f"in_{k}": m for k, m in arrays.items()}], core_ids=[0])
    return r.results[0]["out"][:N]
```

```python
from contextlib import ExitStack, contextmanager

import numpy as np

import concourse.bass as bass
from concourse import mybir

F32 = mybir.dt.float32
F32R = mybir.dt.float32r
BF16 = mybir.dt.bfloat16
I32 = mybir.dt.int32
ACT = mybir.ActivationFunctionType
ALU = mybir.AluOpType
X = mybir.AxisListType.X

P = 128
N, D, E = 10000, 512, 5000
H, DH, DFF, NTYPE = 8, 64, 64, 8
KC = D // P
NT = 80
NP = NT * P
EC = 125
ET = E // EC
SLOTS = ET * P
PER = P - 1
EPS = 1e-5
FAR = -1e30
MAGIC = float(3 << 22)
SRC, DST, TYP, WGT = 0, 1, 2, 3

assert NP >= N + P and ET * PER >= E and SLOTS == ET * P and KC * P == D
assert D == H * DH and EC * ET == E


def host_constants():
    j = np.arange(P, dtype=np.float32)
    iota = np.tile(j, (P, 1))
    part = iota.T
    c = {
        "iota": iota,
        "ident": (iota == part).astype(np.float32),
        "earlier": (iota < part).astype(np.float32),
        "above": (iota > part).astype(np.float32),
        "ones": np.ones((P, P), np.float32),
        "zrow": iota + SLOTS,
    }
    heads = np.zeros((P, KC, H), np.float32)
    for k in range(KC):
        for p in range(P):
            heads[p, k, (k * P + p) // DH] = 1.0
    table = np.zeros((SLOTS, 4), np.float32)
    table[:, SRC] = table[:, DST] = N
    eps = np.full((P, 1), EPS, np.float32)
    packed = np.concatenate([c[k] for k in CONSTS] + [heads.reshape(P, KC * H), part[:, :1], eps], axis=1)
    return np.ascontiguousarray(packed), table


CONSTS = ("iota", "ident", "earlier", "above", "ones", "zrow")
CW = len(CONSTS) * P + KC * H + 2


class Names:
    pass


class Tile:

    def __init__(self, i, b, u):
        self.i, self.b, self.u, self.m = i, b, u, i * u + b

    def back(self, lag):
        return Tile(self.i, self.b - lag, self.u)

    def known(self):
        return isinstance(self.i, int)

    def exists(self, count):
        return not self.known() or 0 <= self.m < count

    def slot(self, ring):
        return self.b % ring

    def turn(self, ring):
        return self.i * (self.u // ring) + self.b // ring

    def reuses(self, ring):
        return not self.known() or self.m >= ring


def tiles(eng, count, lag, body, u=4, peeled=1):
    for b in range(u * peeled):
        body(Tile(b // u, b % u, u))
    with eng.Fori(peeled, count // u) as i:
        for b in range(u):
            body(Tile(i, b, u))
    for b in range(lag):
        body(Tile(count // u, b, u))


class Steps:

    def __init__(self, eng, sem, per):
        self.eng, self.sem, self.per = eng, sem, per

    def tile(self, m):
        self.base, self.k = m * self.per, 0
        return self

    def __call__(self, ins):
        self.last(ins)
        self.eng.wait_ge(self.sem, self.base + self.k)

    def alone(self, ins, passed):
        self(ins)
        self.eng.sem_inc(passed, 1)

    def last(self, ins):
        self.k += 1
        assert self.k <= self.per
        ins.then_inc(self.sem, 1)


@contextmanager
def phase(nc, name):
    with ExitStack() as ctx:
        f = Names()
        f.sems = []

        def sb(n, shape, dt=F32):
            return ctx.enter_context(nc.sbuf_tensor(f"{name}_{n}", shape, dt))

        def psum(n, shape, dt=F32):
            return ctx.enter_context(nc.psum_tensor(f"{name}_ps_{n}", shape, dt))

        def sem(n):
            s = nc.alloc_semaphore(f"{name}_{n}")
            f.sems.append(s)
            return s

        f.sb, f.psum, f.sem = sb, psum, sem
        f.passed_dve, f.passed_pool = sem("passed_dve"), sem("passed_pool")
        with nc.Block() as block:
            f.block = block
            yield f
        nc.clear_and_free_semaphores(f.sems)
        nc.all_engine_barrier()


def rows(ap, m):
    return ap[bass.ts(m, P), :]



def load_constants(nc, s):
    with phase(nc, "const") as f:
        loaded, zeroed, stored = f.sem("loaded"), f.sem("zeroed"), f.sem("stored")
        zeros = f.sb("zeros", [P, D])

        @f.block.sync
        def _(sp):
            sp.dma_start(s.packed[:], s.inputs["consts_dram"]).then_inc(loaded, 16)
            sp.wait_ge(zeroed, 1)
            sp.dma_start(s.edge_out[SLOTS:SLOTS + P, :], zeros[:]).then_inc(stored, 16)
            sp.wait_ge(loaded, 16)
            sp.wait_ge(stored, 16)

        @f.block.vector
        def _(dve):
            nc.vector.memset(zeros[:], 0.0).then_inc(zeroed, 1)


def sort_edges(nc, s, order):
    key = order.key
    G = 4
    with phase(nc, f"sort{key}") as f:
        raw = f.sb("raw", [EC, 3, ET], I32)
        pay = f.sb("pay", [EC, ET, 4])
        weight = f.sb("weight", [EC, ET])
        krow = f.sb("krow", [P, E], I32)
        hirow = f.sb("hirow", [P, E], I32)
        hi_onehot_t = f.sb("hi_onehot_t", [P, E])
        krow_f = f.sb("krow_f", [P, E])
        same = f.sb("same", [EC, E])
        hi_onehot = f.sb("hi_onehot", [EC, ET * P], BF16)
        lo_onehot = f.sb("lo_onehot", [EC, ET * P], BF16)
        digit = f.sb("digit", [EC, 2, ET], I32)
        digit_f = f.sb("digit_f", [EC, 2, ET])
        scan = f.sb("scan", [P, P])
        rowbase = f.sb("rowbase", [P, 1])
        end = f.sb("end", [P, P])
        base = f.sb("base", [P, P])
        table = f.sb("table", [P, 2, P])
        prod = f.sb("prod", [EC, 2, G * P])
        rank = f.sb("rank", [EC, ET])
        tie = f.sb("tie", [EC, ET])
        tmp = f.sb("tmp", [P, 3, P])
        slot_i = f.sb("slot_i", [EC, ET], I32)
        stage_slot = f.sb("stage_slot", [EC, 2], I32)
        stage_pay = f.sb("stage_pay", [EC, 2, 4])
        sorted_col = f.sb("sorted_col", [P, ET, 4])
        kout = f.sb("kout", [ET, P])
        kin = f.sb("kin", [ET, P])
        breaks = f.sb("breaks", [ET, P])
        begin = f.sb("begin", [1, 1])
        ps_total = f.psum("total", [P, 512])
        ps_small = f.psum("small", [P, 512])
        ps_place = f.psum("place", [P, 512])
        ps_key = f.psum("key", [P, 512])
        ps_run = f.psum("run", [P, 512])
        ps_look = [f.psum(f"look{b}", [EC, 512]) for b in range(2)]

        loads, prefilled = f.sem("loads"), f.sem("prefilled")
        cols_ready, total_ready, scanned, rowbase_ready = (
            f.sem("cols_ready"), f.sem("total_ready"), f.sem("scanned"), f.sem("rowbase_ready"))
        onehot_t_ready, table_ready, counted, looked = (
            f.sem("onehot_t_ready"), f.sem("table_ready"), f.sem("counted"), f.sem("looked"))
        summed, places_ready, places_turned = f.sem("summed"), f.sem("places_ready"), f.sem("places_turned")
        slots_ready, staged, sorted_loaded = f.sem("slots_ready"), f.sem("staged"), f.sem("sorted_loaded")
        scattered = [f.sem(f"scattered{b}") for b in range(2)]
        key_turned, kout_ready, kin_written = f.sem("key_turned"), f.sem("kout_ready"), f.sem("kin_written")
        kin_loaded, breaks_ready, written = f.sem("kin_loaded"), f.sem("breaks_ready"), f.sem("written")
        kin_turned = f.sem("kin_turned")
        picked = f.sem("picked")
        chain = f.sem("chain")

        @f.block.sync
        def _(sp):
            sp.dma_start(raw[:, 0, :], s.inputs["src_col"]).then_inc(loads, 16)
            sp.dma_start(raw[:, 1, :], s.inputs["dst_col"]).then_inc(loads, 16)
            sp.dma_start(raw[:, 2, :], s.inputs["type_col"]).then_inc(loads, 16)
            sp.dma_start(weight[:], s.inputs["weight_col"]).then_inc(loads, 16)
            sp.dma_start(krow[:], (s.inputs["dst_flat"] if key == DST else s.inputs["src_flat"]).partition_broadcast(P)).then_inc(loads, 16)
            sp.dma_start(order.table, s.inputs["table_default"]).then_inc(prefilled, 16)
            for b in range(2):
                sp.wait_ge(scattered[b], 16 * (ET // 2))
            sp.dma_start(sorted_col[:], order.table.rearrange("(t p) c -> p t c", p=P)).then_inc(sorted_loaded, 16)
            sp.wait_ge(kout_ready, 2)
            sp.dma_start(order.key_out.rearrange("(t p) -> t p", p=P), kout[:]).then_inc(written, 16)
            sp.dma_start(order.key_in[1:, 0:1], kout[0:ET - 1, P - 1:P], allow_slow_non_contiguous=True).then_inc(kin_written, 16)
            sp.dma_start(order.key_in[0:1, 0:1], begin[:]).then_inc(kin_written, 16)
            sp.dma_start(order.key_in[:, 1:P], kout[:, 1:P]).then_inc(kin_written, 16)
            sp.wait_ge(kin_written, 48)
            sp.dma_start(kin[:], order.key_in).then_inc(kin_loaded, 16)
            sp.wait_ge(breaks_ready, 2)
            sp.dma_start(order.breaks, breaks[:]).then_inc(written, 16)
            sp.wait_ge(written, 32)
            sp.wait_ge(kin_loaded, 16)
            sp.wait_ge(prefilled, 16)

        def look_sum(dve, g):
            dve.wait_ge(looked, (g + 1) * G)
            if g >= 2:
                dve.wait_ge(summed, g - 1)
            nc.vector.tensor_tensor(prod[:, g % 2, :], ps_look[g % 2][:], lo_onehot[:, bass.ts(g, G * P)], ALU.mult).then_inc(picked, 1)
            dve.wait_ge(picked, g + 1)
            nc.vector.tensor_reduce(rank[:, g * G:g * G + G], prod[:, g % 2, :].rearrange("p (t j) -> p t j", j=P),
                                    X, ALU.add).then_inc(summed, 1)

        @f.block.vector
        def _(dve):
            n = [0]

            def link(ins):
                n[0] += 1
                ins.then_inc(chain, 1)
                dve.wait_ge(chain, n[0])

            def slot_of(out, rank_ap, p, n):
                a, b = tmp[0:p, 1, 0:n], tmp[0:p, 2, 0:n]
                link(nc.vector.tensor_scalar(a, rank_ap, 0.5, 1.0 / PER, ALU.add, ALU.mult))
                link(nc.vector.tensor_scalar(b, a, -0.5, None, ALU.add))
                link(nc.vector.tensor_scalar(a, b, MAGIC, None, ALU.add))
                link(nc.vector.tensor_scalar(b, a, MAGIC, 1.0, ALU.subtract, ALU.add))
                link(nc.vector.tensor_tensor(out, rank_ap, b, ALU.add))

            dve.wait_ge(loads, 80)
            kcol = raw[:, key, :]
            link(nc.vector.tensor_scalar(digit[:, 0, :], kcol, 7, None, ALU.logical_shift_right))
            link(nc.vector.tensor_scalar(digit[:, 1, :], kcol, P - 1, None, ALU.bitwise_and))
            link(nc.vector.tensor_copy(digit_f[:], digit[:]))
            wide = [EC, ET, P]
            for g, onehot in ((0, hi_onehot), (1, lo_onehot)):
                nc.vector.tensor_tensor(
                    onehot[:].rearrange("p (t j) -> p t j", j=P), s.iota[0:EC, :].unsqueeze(1).to_broadcast(wide),
                    digit_f[:, g, :].unsqueeze(2).to_broadcast(wide), ALU.is_equal).then_inc(cols_ready, 1)
            for c in (SRC, DST, TYP):
                link(nc.vector.tensor_copy(pay[:, :, c], raw[:, c, :]))
            link(nc.vector.tensor_copy(pay[:, :, WGT], weight[:]))
            link(nc.vector.tensor_scalar(hirow[:], krow[:], 7, None, ALU.logical_shift_right))
            nc.vector.tensor_scalar(hi_onehot_t[:], hirow[:], s.part, None, ALU.is_equal).then_inc(onehot_t_ready, 1)
            link(nc.vector.tensor_copy(krow_f[:], krow[:]))

            dve.wait_ge(total_ready, 1)
            nc.vector.tensor_tensor_scan(scan[:], s.ones, ps_total[:, 0:P], 0.0, ALU.mult, ALU.add).then_inc(scanned, 1)
            dve.wait_ge(rowbase_ready, 1)
            link(nc.vector.tensor_copy(rowbase[:], ps_small[:, 0:1]))
            dve.wait_ge(scanned, 1)
            link(nc.vector.tensor_scalar(end[:], scan[:], rowbase[:], None, ALU.add))
            link(nc.vector.tensor_tensor(base[:], end[:], ps_total[:, 0:P], ALU.subtract))

            for g in range(ET // G):
                for t in range(g * G, g * G + G):
                    if t >= 2:
                        dve.wait_ge(looked, t - 1)
                    if t == 0:
                        nc.vector.tensor_copy(table[:, 0, :], base[:]).then_inc(table_ready, 1)
                    else:
                        dve.wait_ge(counted, t)
                        nc.vector.tensor_tensor(table[:, t % 2, :], base[:], ps_run[:, 0:P], ALU.add).then_inc(table_ready, 1)
                if g >= 1:
                    look_sum(dve, g - 1)
            look_sum(dve, ET // G - 1)

            cube = [EC, ET, EC]
            same3 = same[:].rearrange("p (t j) -> p t j", j=EC)
            kcol_f = pay[:, :, key].unsqueeze(2).to_broadcast(cube)
            link(nc.vector.tensor_tensor(same3, krow_f[0:EC, :].rearrange("p (t j) -> p t j", j=EC), kcol_f, ALU.is_equal))
            link(nc.vector.tensor_tensor(same3, same3, s.earlier[0:EC, 0:EC].unsqueeze(1).to_broadcast(cube), ALU.mult))
            link(nc.vector.tensor_reduce(tie[:], same3, X, ALU.add))
            dve.wait_ge(summed, ET // G)
            link(nc.vector.tensor_tensor(rank[:], rank[:], tie[:], ALU.add))
            slot_of(tmp[0:EC, 0, 0:ET], rank[:], EC, ET)
            nc.vector.tensor_copy(slot_i[:], tmp[0:EC, 0, 0:ET]).then_inc(slots_ready, 1)
            dve.wait_ge(slots_ready, 1)

            last = scan[:]
            link(nc.vector.tensor_scalar(last, end[:], -1.0, None, ALU.add))
            slot_of(tmp[:, 0, :], last, P, P)
            link(nc.vector.tensor_tensor(tmp[:, 0, :], tmp[:, 0, :], s.zrow, ALU.subtract))
            link(nc.vector.tensor_scalar(tmp[:, 1, :], ps_total[:, 0:P], 0.0, None, ALU.is_gt))
            link(nc.vector.tensor_tensor(tmp[:, 0, :], tmp[:, 0, :], tmp[:, 1, :], ALU.mult))
            nc.vector.tensor_tensor(tmp[:, 2, :], tmp[:, 0, :], s.zrow, ALU.add).then_inc(places_ready, 1)
            dve.wait_ge(places_turned, 1)
            link(nc.vector.tensor_copy(order.place[:], ps_place[:, 0:NT]))

            dve.wait_ge(sorted_loaded, 16)
            other = SRC + DST - key
            link(nc.vector.tensor_copy(order.other_idx[:], sorted_col[:, :, other]))
            link(nc.vector.tensor_copy(order.key_idx[:], sorted_col[:, :, key]))
            link(nc.vector.tensor_copy(order.type_col[:], sorted_col[:, :, TYP]))
            link(nc.vector.tensor_copy(order.weight_col[:], sorted_col[:, :, WGT]))
            nc.vector.memset(begin[:], -1.0).then_inc(kout_ready, 1)
            dve.wait_ge(key_turned, 1)
            link(nc.vector.tensor_copy(kout[:], ps_key[0:ET, 0:P]))
            nc.vector.tensor_copy(kout[:, 0:1], kout[:, P - 1:P]).then_inc(kout_ready, 1)
            dve.wait_ge(kin_loaded, 16)
            nc.vector.memset(breaks[:, 0:1], 0.0).then_inc(breaks_ready, 1)
            link(nc.vector.tensor_tensor(breaks[:, 1:P], kin[:, 1:P], kin[:, 0:P - 1], ALU.not_equal))
            nc.vector.tensor_scalar(breaks[:, 1:P], breaks[:, 1:P], FAR, None, ALU.mult).then_inc(breaks_ready, 1)
            dve.wait_ge(kin_turned, 1)
            link(nc.vector.tensor_copy(order.key_in_col[:], ps_small[:, 0:ET]))


        @f.block.tensor
        def _(pe):
            pe.wait_ge(cols_ready, 2)
            for t in range(ET):
                mm = pe.matmul(ps_total[:, 0:P], hi_onehot[:, bass.ts(t, P)], lo_onehot[:, bass.ts(t, P)],
                               start=t == 0, stop=t == ET - 1)
            mm.then_inc(total_ready, 1)
            pe.wait_ge(scanned, 1)
            pe.matmul(ps_small[:, 0:1], s.above, scan[:, P - 1:P], start=True, stop=True).then_inc(rowbase_ready, 1)
            pe.wait_ge(onehot_t_ready, 1)
            for t in range(ET):
                g = t // G
                pe.wait_ge(table_ready, t + 1)
                if t < ET - 1:
                    pe.matmul(ps_run[:, 0:P], hi_onehot[:, bass.ts(t, P)], lo_onehot[:, bass.ts(t, P)],
                              start=t == 0, stop=True, skip_group_check=True).then_inc(counted, 1)
                if g >= 2 and t % G == 0:
                    pe.wait_ge(picked, g - 1)
                pe.matmul(ps_look[g % 2][:, bass.ts(t % G, P)], hi_onehot_t[:, bass.ts(t, EC)], table[:, t % 2, :],
                          start=True, stop=True).then_inc(looked, 1)
            pe.wait_ge(places_ready, 1)
            pe.transpose(ps_place[:, 0:P], tmp[:, 2, :], s.ident).then_inc(places_turned, 1)
            pe.wait_ge(sorted_loaded, 16)
            pe.transpose(ps_key[0:ET, 0:P], sorted_col[:, :, key], s.ident).then_inc(key_turned, 1)
            pe.wait_ge(kin_loaded, 16)
            pe.transpose(ps_small[:, 0:ET], kin[:], s.ident[0:ET, 0:ET]).then_inc(kin_turned, 1)

        @f.block.gpsimd
        def _(pool):
            pool.wait_ge(slots_ready, 1)
            pool.wait_ge(prefilled, 16)
            with pool.Fori(0, ET // 2) as i:
                for b in range(2):
                    pool.wait_ge(scattered[b], i * 16)
                    nc.gpsimd.tensor_copy(stage_slot[:, b:b + 1], slot_i[:, bass.ds(i * 2 + b, 1)]).then_inc(staged, 1)
                    nc.gpsimd.tensor_copy(stage_pay[:, b, :], pay[:].rearrange("p t c -> p (t c)")[:, bass.ts(i * 2 + b, 4)]).then_inc(staged, 1)
                    pool.wait_ge(staged, i * 4 + 2 * b + 2)
                    pool.sem_inc(f.passed_pool, 1)
                    nc.gpsimd.indirect_dma_start(
                        out=order.table, out_offset=bass.IndirectOffsetOnAxis(ap=stage_slot[:, b:b + 1], axis=0),
                        in_=stage_pay[:, b, :], in_offset=None).then_inc(scattered[b], 16)



class Weights:

    def __init__(self, f, named, scales=None):
        self.named, self.scales = named, scales or {}
        self.stage = f.sb("w_stage", [P, 2, KC * D])
        self.hi = {k: f.sb(f"{k}_hi", [P, KC * w], F32R) for k, (_, w) in named.items()}
        self.lo = {k: f.sb(f"{k}_lo", [P, KC * w], F32R) for k, (_, w) in named.items()}
        self.loaded = [f.sem(f"w_loaded{b}") for b in range(2)]
        self.scaled, self.hi_done, self.lo_done = f.sem("w_scaled"), f.sem("w_hi"), f.sem("w_lo")
        self.count = len(named)

    def load(self, sp):
        for j, (src, w) in enumerate(self.named.values()):
            if j >= 2:
                sp.wait_ge(self.lo_done, j - 1)
            sp.dma_start(self.stage[:, j % 2, 0:KC * w].rearrange("p (k n) -> p k n", n=w),
                         src.rearrange("(k p) n -> p k n", p=P)).then_inc(self.loaded[j % 2], 16)

    def split_hi(self, nc, act):
        for j, (name, (_, w)) in enumerate(self.named.items()):
            act.wait_ge(self.loaded[j % 2], 16 * (j // 2 + 1))
            if self.scales:
                act.wait_ge(self.scaled, KC * (j + 1))
            nc.scalar.activation(self.hi[name][:], self.stage[:, j % 2, 0:KC * w], ACT.Copy).then_inc(self.hi_done, 1)

    def split_lo(self, nc, dve):
        for j, (name, (_, w)) in enumerate(self.named.items()):
            stage = self.stage[:, j % 2, 0:KC * w]
            if self.scales:
                dve.wait_ge(self.loaded[j % 2], 16 * (j // 2 + 1))
                for k in range(KC):
                    nc.vector.tensor_scalar(stage[:, bass.ts(k, w)], stage[:, bass.ts(k, w)],
                                            self.scales[name][:, k:k + 1], None, ALU.mult).then_inc(self.scaled, 1)
            dve.wait_ge(self.hi_done, j + 1)
            nc.vector.tensor_tensor(self.lo[name][:], stage, self.hi[name][:].bitcast(F32), ALU.subtract).then_inc(self.lo_done, 1)

    def product(self, pe, out, hi, lo, name):
        w = self.named[name][1]
        for k in range(KC):
            for j, (a, b) in enumerate(((hi, self.hi), (hi, self.lo), (lo, self.hi))):
                mm = pe.matmul(out, a[:, bass.ts(k, P)], b[name][:, bass.ts(k, w)],
                               start=k == 0 and j == 0, stop=k == KC - 1 and j == 2)
        return mm


def transpose_tile(pe, out, tile, ident):
    for k in range(KC):
        mm = pe.transpose(out[:, bass.ts(k, P)], tile[:, bass.ts(k, P)], ident)
    return mm


def norm_stats(nc, steps, passed, stats, mv, x):
    steps.alone(nc.vector.bn_stats(stats, x), passed)
    steps.last(nc.vector.bn_aggr(mv, stats))


def deviation(nc, s, out, mv):
    return nc.scalar.activation(out, mv[:, 1:2], ACT.Sqrt, bias=s.eps)


def norm_scale(nc, steps, mv, dev, rstd):
    steps(nc.vector.reciprocal(rstd[:, 0:1], dev))
    steps.last(nc.vector.tensor_scalar(rstd[:, 1:2], mv[:, 0:1], rstd[:, 0:1], -1.0, ALU.mult, ALU.mult))


def gather(nc, pool, passed, staged, t, idx, stage, table, out, done):
    nc.gpsimd.tensor_copy(stage, idx[:, bass.ds(t.m, 1)]).then_inc(staged[0], 1)
    pool.wait_ge(staged[0], t.m * staged[1] + staged[2])
    pool.sem_inc(passed, 1)
    nc.gpsimd.indirect_dma_start(out=out, out_offset=None, in_=table,
                                 in_offset=bass.IndirectOffsetOnAxis(ap=stage, axis=0)).then_inc(done, 16)



def dense_root(nc, s):
    with phase(nc, "root") as f:
        gcol, bcol = f.sb("gcol", [P, KC]), f.sb("bcol", [P, KC])
        brows = f.sb("brows", [P, KC * P])
        bl = f.sb("bl", [P, D])
        wr_plain = f.sb("wr_plain", [P, KC * D])
        bias = f.sb("bias", [P, D])
        W = Weights(f, {"wr": (s.inputs["wr_t"], D)}, {"wr": gcol})
        x = f.sb("x", [P, 4, D])
        z = f.sb("z", [P, 2, D])
        hi, lo = f.sb("hi", [P, 2, D], F32R), f.sb("lo", [P, 2, D], F32R)
        u = f.sb("u", [P, 2, D])
        stats, mv, dev, rstd = f.sb("stats", [P, 2, 6]), f.sb("mv", [P, 2, 2]), f.sb("dev", [P, 2, 1]), f.sb("rstd", [P, 2, 1])
        dev_done = f.sem("dev_done")
        ps_t = [f.psum(f"t{b}", [P, D]) for b in range(2)]
        ps_o = [f.psum(f"o{b}", [P, D]) for b in range(2)]
        params, brows_ready, bias_made, bias_ready = f.sem("params"), f.sem("brows"), f.sem("bias_made"), f.sem("bias_ready")
        x_loaded = [f.sem(f"x_loaded{b}") for b in range(4)]
        u_stored = [f.sem(f"u_stored{b}") for b in range(2)]
        norm, turned, hi_done, lo_done, mm_done, u_ready = (f.sem(n) for n in (
            "norm", "turned", "hi_done", "lo_done", "mm_done", "u_ready"))

        @f.block.sync
        def _(sp):
            sp.dma_start(gcol[:], s.inputs["ln0_g_col"]).then_inc(params, 16)
            sp.dma_start(bcol[:], s.inputs["ln0_b_col"]).then_inc(params, 16)
            sp.dma_start(bl[:], s.inputs["b_l"].partition_broadcast(P)).then_inc(params, 16)
            sp.dma_start(wr_plain[:].rearrange("p (k n) -> p k n", n=D),
                         s.inputs["wr_t"].rearrange("(k p) n -> p k n", p=P)).then_inc(params, 16)
            W.load(sp)

            def step(t):
                if t.exists(NT):
                    if t.reuses(4):
                        sp.wait_ge(norm, 4 * (t.m - 3))
                    sp.dma_start(x[:, t.slot(4), :], rows(s.inputs["x"], t.m)).then_inc(x_loaded[t.slot(4)], 16)
                t = t.back(4)
                if t.exists(NT):
                    sp.wait_ge(u_ready, t.m + 1)
                    sp.dma_start(rows(s.root, t.m), u[:, t.slot(2), :]).then_inc(u_stored[t.slot(2)], 16)
            tiles(sp, NT, 4, step)
            for b in range(2):
                sp.wait_ge(u_stored[b], 16 * (NT // 2))

        @f.block.vector
        def _(dve):
            steps = Steps(dve, norm, 4)
            dve.wait_ge(params, 64)
            for k in range(KC):
                nc.vector.tensor_scalar(brows[:, bass.ts(k, P)], s.ones, bcol[:, k:k + 1], None, ALU.mult).then_inc(brows_ready, 1)
            W.split_lo(nc, dve)
            dve.wait_ge(bias_made, 1)
            nc.vector.tensor_tensor(bias[:], bl[:], ps_o[0][:], ALU.add).then_inc(bias_ready, 1)

            def step(t):
                if t.exists(NT):
                    b = t.slot(2)
                    xt = x[:, t.slot(4), :]
                    st = steps.tile(t.m)
                    dve.wait_ge(x_loaded[t.slot(4)], 16 * t.turn(4) + 16)
                    norm_stats(nc, st, f.passed_dve, stats[:, b, :], mv[:, b, :], xt)
                now = t
                t = t.back(1)
                if t.exists(NT):
                    b = t.slot(2)
                    dve.wait_ge(hi_done, t.m + 1)
                    nc.vector.tensor_tensor(lo[:, b, :], ps_t[b][:], hi[:, b, :].bitcast(F32), ALU.subtract).then_inc(lo_done, 1)
                t = t.back(1)
                if t.exists(NT):
                    b = t.slot(2)
                    dve.wait_ge(mm_done, t.m + 1)
                    if t.reuses(2):
                        dve.wait_ge(u_stored[b], 16 * t.turn(2))
                    else:
                        dve.wait_ge(bias_ready, 1)
                    nc.vector.tensor_tensor(u[:, b, :], ps_o[b][:], bias[:], ALU.add).then_inc(u_ready, 1)
                t = now
                if t.exists(NT):
                    b = t.slot(2)
                    dve.wait_ge(dev_done, t.m + 1)
                    st(nc.vector.reciprocal(rstd[:, b, :], dev[:, b, :]))
                    if t.reuses(2):
                        dve.wait_ge(turned, t.m - 1)
                    st.last(nc.vector.tensor_scalar(z[:, b, :], xt, mv[:, b, 0:1], rstd[:, b, :], ALU.subtract, ALU.mult))
            tiles(dve, NT, 2, step)

        @f.block.scalar
        def _(act):
            nc.scalar.preload_act_table(ACT.Sqrt)
            W.split_hi(nc, act)

            def step(t):
                if t.exists(NT):
                    b = t.slot(2)
                    act.wait_ge(norm, 4 * t.m + 2)
                    deviation(nc, s, dev[:, b, :], mv[:, b, :]).then_inc(dev_done, 1)
                    act.wait_ge(turned, t.m + 1)
                    if t.reuses(2):
                        act.wait_ge(mm_done, t.m - 1)
                    nc.scalar.activation(hi[:, b, :], ps_t[b][:], ACT.Copy).then_inc(hi_done, 1)
            tiles(act, NT, 0, step)

        @f.block.tensor
        def _(pe):
            pe.wait_ge(brows_ready, KC)
            for k in range(KC):
                mm = pe.matmul(ps_o[0][:], brows[:, bass.ts(k, P)], wr_plain[:, bass.ts(k, D)], start=k == 0, stop=k == KC - 1)
            mm.then_inc(bias_made, 1)
            pe.wait_ge(W.lo_done, W.count)
            pe.wait_ge(bias_ready, 1)

            def step(t):
                if t.exists(NT):
                    b = t.slot(2)
                    pe.wait_ge(norm, 4 * t.m + 4)
                    if t.reuses(2):
                        pe.wait_ge(lo_done, t.m - 1)
                    transpose_tile(pe, ps_t[b], z[:, b, :], s.ident).then_inc(turned, 1)
                t = t.back(1)
                if t.exists(NT):
                    b = t.slot(2)
                    pe.wait_ge(lo_done, t.m + 1)
                    if t.reuses(2):
                        pe.wait_ge(u_ready, t.m - 1)
                    W.product(pe, ps_o[b][:], hi[:, b, :], lo[:, b, :], "wr").then_inc(mm_done, 1)
            tiles(pe, NT, 1, step)



def aggregate(nc, s, order, name, values=None, weights=None, source=None, matrix=None, small=0.0):
    mean = source is not None
    ZW = 1 if mean else H
    with phase(nc, name) as f:
        key_out = f.sb("key_out", [P, SLOTS])
        v = f.sb("v", [P, 2, D + ZW])
        sel = f.sb("sel", [P, 2, P])
        a = f.sb("a", [P, 2, D])
        rz = f.sb("rz", [P, 2, 2 * H])
        zero = f.sb("zero", [1, D])
        ps_r = [f.psum(f"r{b}", [P, D]) for b in range(2)]
        ps_z = [f.psum(f"z{b}", [P, 512]) for b in range(2)]
        setup, zeroed = f.sem("setup"), f.sem("zeroed")
        v_steps, sel_ready, carried, summed = f.sem("v_steps"), f.sem("sel_ready"), f.sem("carried"), f.sem("summed")
        a_steps, turned, hi_done, lo_done, mm_done, o_ready = (f.sem(n) for n in (
            "a_steps", "turned", "hi_done", "lo_done", "mm_done", "o_ready"))
        stored = [f.sem(f"stored{b}") for b in range(2)]
        if mean:
            x = f.sb("x", [P, 4, D])
            stage = f.sb("stage", [P, 4], I32)
            stats, mv, dev, rstd = f.sb("stats", [P, 2, 6]), f.sb("mv", [P, 2, 2]), f.sb("dev", [P, 2, 1]), f.sb("rstd", [P, 2, 1])
            dev_done = f.sem("dev_done")
            gathered = [f.sem(f"gathered{b}") for b in range(4)]
            staged = f.sem("staged")
            gcol, bcol = f.sb("gcol", [P, KC]), f.sb("bcol", [P, KC])
            brows = f.sb("brows", [P, KC * P])
            plain = f.sb("plain", [P, KC * D])
            bias = f.sb("bias", [P, D])
            brows_ready, bias_made, bias_ready = f.sem("brows"), f.sem("bias_made"), f.sem("bias_ready")
        if matrix is not None:
            W = Weights(f, {"w": (matrix, D)}, {"w": gcol} if mean else None)
            hi, lo = f.sb("hi", [P, 2, D], F32R), f.sb("lo", [P, 2, D], F32R)
            o = f.sb("o", [P, 2, D])
            ps_t = [f.psum(f"t{b}", [P, D]) for b in range(2)]
            ps_o = [f.psum(f"o{b}", [P, D]) for b in range(2)]
        VS = 4 if mean else 2
        AS = 2 if small == 0.0 else 3
        out_lag = 4 if matrix is not None else 2

        @f.block.sync
        def _(sp):
            sp.dma_start(key_out[:], order.key_out.partition_broadcast(P)).then_inc(setup, 16)
            if mean:
                sp.dma_start(gcol[:], s.inputs["ln0_g_col"]).then_inc(setup, 16)
                sp.dma_start(bcol[:], s.inputs["ln0_b_col"]).then_inc(setup, 16)
                sp.dma_start(plain[:].rearrange("p (k n) -> p k n", n=D),
                             matrix.rearrange("(k p) n -> p k n", p=P)).then_inc(setup, 16)
            if matrix is not None:
                W.load(sp)

            def step(t):
                t = t.back(out_lag)
                if t.exists(ET):
                    b = t.slot(2)
                    if matrix is not None:
                        sp.wait_ge(o_ready, t.m + 1)
                        res = o[:, b, :]
                    else:
                        sp.wait_ge(a_steps, AS * t.m + AS)
                        res = a[:, b, :]
                    sp.dma_start(rows(s.edge_out, t.m), res).then_inc(stored[b], 16)
            tiles(sp, ET, out_lag, step)
            for b in range(2):
                sp.wait_ge(stored[b], 16 * (ET // 2))

        if mean:
            @f.block.gpsimd
            def _(pool):
                def step(t):
                    r = t.slot(4)
                    if t.reuses(4):
                        pool.wait_ge(v_steps, VS * (t.m - 3))
                        pool.wait_ge(gathered[r], 16 * t.turn(4))
                    gather(nc, pool, f.passed_pool, (staged, 1, 1), t, order.other_idx, stage[:, r:r + 1], source, x[:, r, :], gathered[r])
                tiles(pool, ET, 0, step)

        @f.block.vector
        def _(dve):
            vs, asteps = Steps(dve, v_steps, VS), Steps(dve, a_steps, AS)
            nc.vector.memset(zero[:], 0.0).then_inc(zeroed, 1)
            if mean:
                nc.vector.memset(v[:, :, D:D + 1], 1.0).then_inc(zeroed, 1)
                dve.wait_ge(setup, 64)
                for k in range(KC):
                    nc.vector.tensor_scalar(brows[:, bass.ts(k, P)], s.ones, bcol[:, k:k + 1], None, ALU.mult).then_inc(brows_ready, 1)
            if matrix is not None:
                W.split_lo(nc, dve)
            if mean:
                dve.wait_ge(bias_made, 1)
                nc.vector.tensor_copy(bias[:], ps_o[0][:]).then_inc(bias_ready, 1)
                dve.wait_ge(bias_ready, 1)

            def divide(t):
                if not t.exists(ET):
                    return
                b = t.slot(2)
                st = asteps.tile(t.m)
                z = ps_z[b][:, 0:ZW]
                dve.wait_ge(summed, t.m + 1)
                if not (t.known() and t.m == ET - 1):
                    dve.wait_ge(carried, 2 * t.m + 4)
                if small:
                    st(nc.vector.tensor_scalar(rz[:, b, H:H + ZW], z, small, None, ALU.add))
                    z = rz[:, b, H:H + ZW]
                st(nc.vector.reciprocal(rz[:, b, 0:ZW], z))
                if t.reuses(2):
                    if matrix is not None:
                        dve.wait_ge(turned, t.m - 1)
                    else:
                        dve.wait_ge(stored[b], 16 * t.turn(2))
                if mean:
                    st.last(nc.vector.tensor_scalar(a[:, b, :], ps_r[b][:], rz[:, b, 0:1], None, ALU.mult))
                else:
                    st.last(nc.vector.tensor_tensor(
                        a[:, b, :].rearrange("p (h d) -> p h d", d=DH), ps_r[b][:].rearrange("p (h d) -> p h d", d=DH),
                        rz[:, b, 0:H].unsqueeze(2).to_broadcast([P, H, DH]), ALU.mult))

            def step(t):
                now, before = t, t.back(1)
                if mean and now.exists(ET):
                    b = now.slot(2)
                    xt = x[:, now.slot(4), :]
                    st = vs.tile(now.m)
                    dve.wait_ge(gathered[now.slot(4)], 16 * now.turn(4) + 16)
                    norm_stats(nc, st, f.passed_dve, stats[:, b, :], mv[:, b, :], xt)
                if now.exists(ET):
                    b = now.slot(2)
                    if now.known() and now.m == 0:
                        dve.wait_ge(setup, 64 if mean else 16)
                    if mean:
                        dve.wait_ge(dev_done, now.m + 1)
                        st(nc.vector.reciprocal(rstd[:, b, :], dev[:, b, :]))
                        if now.reuses(2):
                            dve.wait_ge(summed, now.m - 1)
                        st.last(nc.vector.tensor_scalar(v[:, b, 0:D], xt, mv[:, b, 0:1], rstd[:, b, :], ALU.subtract, ALU.mult))
                    else:
                        st = vs.tile(now.m)
                        if now.reuses(2):
                            dve.wait_ge(summed, now.m - 1)
                        w = weights[:, bass.ts(now.m, H)]
                        st.last(nc.vector.tensor_tensor(
                            v[:, b, 0:D].rearrange("p (h d) -> p h d", d=DH), values[:, bass.ts(now.m, D)].rearrange("p (h d) -> p h d", d=DH),
                            w.unsqueeze(2).to_broadcast([P, H, DH]), ALU.mult))
                        st.last(nc.vector.tensor_copy(v[:, b, D:D + H], w))
                    nc.vector.tensor_scalar(sel[:, b, :], key_out[:, bass.ts(now.m, P)], order.key_in_col[:, bass.ds(now.m, 1)],
                                            None, ALU.is_equal).then_inc(sel_ready, 1)
                divide(before)
                t = before
                if matrix is None:
                    return
                t = t.back(1)
                if t.exists(ET):
                    b = t.slot(2)
                    dve.wait_ge(hi_done, t.m + 1)
                    nc.vector.tensor_tensor(lo[:, b, :], ps_t[b][:], hi[:, b, :].bitcast(F32), ALU.subtract).then_inc(lo_done, 1)
                t = t.back(1)
                if mean and t.exists(ET):
                    b = t.slot(2)
                    dve.wait_ge(mm_done, t.m + 1)
                    if t.reuses(2):
                        dve.wait_ge(stored[b], 16 * t.turn(2))
                    nc.vector.tensor_tensor(o[:, b, :], ps_o[b][:], bias[:], ALU.add).then_inc(o_ready, 1)
            tiles(dve, ET, 1 if matrix is None else 3, step)

        @f.block.scalar
        def _(act):
            if mean:
                nc.scalar.preload_act_table(ACT.Sqrt)
            if matrix is not None:
                W.split_hi(nc, act)

            def step(t):
                if mean and t.exists(ET):
                    b = t.slot(2)
                    act.wait_ge(v_steps, VS * t.m + 2)
                    deviation(nc, s, dev[:, b, :], mv[:, b, :]).then_inc(dev_done, 1)
                if t.exists(ET):
                    b, before = t.slot(2), t.back(1).slot(2)
                    act.wait_ge(v_steps, VS * t.m + VS)
                    if t.known() and t.m == 0:
                        act.wait_ge(zeroed, 2 if mean else 1)
                        r, z = zero[0:1, 0:D], zero[0:1, 0:ZW]
                    else:
                        act.wait_ge(summed, t.m)
                        r, z = ps_r[before][0:1, :], ps_z[before][0:1, 0:ZW]
                    nc.scalar.activation(v[0:1, b, 0:D], r, ACT.Copy).then_inc(carried, 1)
                    nc.scalar.activation(v[0:1, b, D:D + ZW], z, ACT.Copy).then_inc(carried, 1)
                if matrix is None:
                    return
                t = t.back(1)
                if t.exists(ET):
                    b = t.slot(2)
                    act.wait_ge(turned, t.m + 1)
                    if t.reuses(2):
                        act.wait_ge(mm_done, t.m - 1)
                    nc.scalar.activation(hi[:, b, :], ps_t[b][:], ACT.Copy).then_inc(hi_done, 1)
                t = t.back(2)
                if not mean and t.exists(ET):
                    b = t.slot(2)
                    act.wait_ge(mm_done, t.m + 1)
                    if t.reuses(2):
                        act.wait_ge(stored[b], 16 * t.turn(2))
                    nc.scalar.activation(o[:, b, :], ps_o[b][:], ACT.Copy).then_inc(o_ready, 1)
            tiles(act, ET, 0 if matrix is None else (1 if mean else 3), step)

        @f.block.tensor
        def _(pe):
            if mean:
                pe.wait_ge(setup, 64)
                pe.wait_ge(brows_ready, KC)
                for k in range(KC):
                    mm = pe.matmul(ps_o[0][:], brows[:, bass.ts(k, P)], plain[:, bass.ts(k, D)], start=k == 0, stop=k == KC - 1)
                mm.then_inc(bias_made, 1)
                pe.wait_ge(bias_ready, 1)
            if matrix is not None:
                pe.wait_ge(W.lo_done, W.count)

            def step(t):
                if t.exists(ET):
                    b = t.slot(2)
                    pe.wait_ge(sel_ready, t.m + 1)
                    pe.wait_ge(carried, 2 * t.m + 2)
                    if t.reuses(2):
                        pe.wait_ge(a_steps, AS * (t.m - 1))
                    pe.matmul(ps_r[b][:], sel[:, b, :], v[:, b, 0:D], start=True, stop=True)
                    pe.matmul(ps_z[b][:, 0:ZW], sel[:, b, :], v[:, b, D:D + ZW], start=True, stop=True).then_inc(summed, 1)
                if matrix is None:
                    return
                t = t.back(1)
                if t.exists(ET):
                    b = t.slot(2)
                    pe.wait_ge(a_steps, AS * t.m + AS)
                    if t.reuses(2):
                        pe.wait_ge(lo_done, t.m - 1)
                    transpose_tile(pe, ps_t[b], a[:, b, :], s.ident).then_inc(turned, 1)
                t = t.back(1)
                if t.exists(ET):
                    b = t.slot(2)
                    pe.wait_ge(lo_done, t.m + 1)
                    if t.reuses(2):
                        pe.wait_ge(o_ready, t.m - 1)
                    W.product(pe, ps_o[b][:], hi[:, b, :], lo[:, b, :], "w").then_inc(mm_done, 1)
            tiles(pe, ET, 0 if matrix is None else 2, step)



def edge_products(nc, s, order, name, table, w_other, w_key, values, scores, dots=None):
    attention = dots is None
    with phase(nc, name) as f:
        W = Weights(f, {**w_other, **w_key})
        xo, xk = f.sb("xo", [P, 2, D]), f.sb("xk", [P, 2, D])
        stage = f.sb("stage", [P, 4], I32)
        part = {(w, h): f.sb(f"x_{w}_{h}", [P, 2, D], F32R) for w in "ok" for h in ("hi", "lo")}
        ps_t = {(w, b): f.psum(f"t{w}{b}", [P, D]) for w in "ok" for b in range(2)}
        staged = f.sem("staged")
        g_other = [f.sem(f"g_other{b}") for b in range(2)]
        g_key = [f.sem(f"g_key{b}") for b in range(2)]
        turned, hi_done, lo_done, v_done, v_read = (f.sem(n) for n in ("turned", "hi_done", "lo_done", "v_done", "v_read"))
        s_done, s_read = f.sem("s_done"), f.sem("s_read")
        if attention:
            q = f.sb("q", [P, 2, D])
            prod = f.sb("prod", [P, 2, D])
            ps_q, ps_k, ps_v = f.psum("q", [P, D]), f.psum("k", [P, D]), f.psum("v", [P, D])
            q_done, k_done, q_read, k_read = (f.sem(n) for n in ("q_done", "k_done", "q_read", "k_read"))
        else:
            ps_v, ps_s = f.psum("v", [P, D]), f.psum("s", [P, D])
            w_nat = f.sb("w_nat", [P, KC * D])
            acol = f.sb("acol", [P, 2, KC])
            blocks = f.sb("blocks", [P, 2, KC, H])
            dhi, dlo = f.sb("dhi", [P, 2, KC * H], F32R), f.sb("dlo", [P, 2, KC * H], F32R)
            ps_d = f.psum("d", [P, D])
            d_loaded, blocks_ready, d_done, d_hi, d_lo = (f.sem(n) for n in ("d_loaded", "blocks_ready", "d_done", "d_hi", "d_lo"))

        @f.block.sync
        def _(sp):
            W.load(sp)
            if not attention:
                sp.dma_start(w_nat[:].rearrange("p (k n) -> p k n", n=D),
                             s.inputs[dots[0]].rearrange("(k p) n -> p k n", p=P)).then_inc(d_loaded, 16)
                sp.dma_start(acol[:, 0, :], s.inputs[dots[1]]).then_inc(d_loaded, 16)
                sp.dma_start(acol[:, 1, :], s.inputs[dots[2]]).then_inc(d_loaded, 16)

        @f.block.gpsimd
        def _(pool):
            def step(t):
                r = t.slot(2)
                if t.reuses(2):
                    pool.wait_ge(turned, 2 * (t.m - 1))
                    pool.wait_ge(g_other[r], 16 * t.turn(2))
                    pool.wait_ge(g_key[r], 16 * t.turn(2))
                gather(nc, pool, f.passed_pool, (staged, 2, 1), t, order.other_idx, stage[:, r:r + 1], table, xo[:, r, :], g_other[r])
                gather(nc, pool, f.passed_pool, (staged, 2, 2), t, order.key_idx, stage[:, 2 + r:3 + r], table, xk[:, r, :], g_key[r])
            tiles(pool, ET, 0, step)

        @f.block.vector
        def _(dve):
            W.split_lo(nc, dve)
            if not attention:
                dve.wait_ge(d_loaded, 48)
                for w in range(2):
                    nc.vector.tensor_tensor(blocks[:, w, :, :], s.heads, acol[:, w, :].unsqueeze(2).to_broadcast([P, KC, H]),
                                            ALU.mult).then_inc(blocks_ready, 1)
                dve.wait_ge(d_hi, 1)
                nc.vector.tensor_tensor(dlo[:].rearrange("p w n -> p (w n)"), ps_d[:, 0:2 * KC * H],
                                        dhi[:].rearrange("p w n -> p (w n)").bitcast(F32), ALU.subtract).then_inc(d_lo, 1)

            def step(t):
                if t.exists(ET):
                    b = t.slot(2)
                    for j, w in enumerate("ok"):
                        dve.wait_ge(hi_done, 2 * t.m + 1 + j)
                        nc.vector.tensor_tensor(part[w, "lo"][:, b, :], ps_t[w, b][:], part[w, "hi"][:, b, :].bitcast(F32),
                                                ALU.subtract).then_inc(lo_done, 1)
                t = t.back(1)
                if t.exists(ET):
                    b = t.slot(2)
                    out = scores[:, bass.ts(t.m, H)]
                    if attention:
                        dve.wait_ge(q_read, t.m + 1)
                        dve.wait_ge(k_done, t.m + 1)
                        nc.vector.tensor_tensor(prod[:, b, :], ps_k[:], q[:, b, :], ALU.mult).then_inc(k_read, 1)
                        dve.wait_ge(k_read, t.m + 1)
                        nc.vector.tensor_reduce(out, prod[:, b, :].rearrange("p (h d) -> p h d", d=DH), X, ALU.add).then_inc(s_read, 1)
                    else:
                        dve.wait_ge(s_done, t.m + 1)
                        nc.vector.tensor_copy(out, ps_s[:, 0:H]).then_inc(s_read, 1)
            tiles(dve, ET, 1, step)

        @f.block.scalar
        def _(act):
            W.split_hi(nc, act)
            if not attention:
                act.wait_ge(d_done, 1)
                nc.scalar.activation(dhi[:].rearrange("p w n -> p (w n)"), ps_d[:, 0:2 * KC * H], ACT.Copy).then_inc(d_hi, 1)

            def step(t):
                if t.exists(ET):
                    b = t.slot(2)
                    for j, w in enumerate("ok"):
                        act.wait_ge(turned, 2 * t.m + 1 + j)
                        if t.reuses(2):
                            act.wait_ge(v_done, t.m - 1)
                        nc.scalar.activation(part[w, "hi"][:, b, :], ps_t[w, b][:], ACT.Copy).then_inc(hi_done, 1)
                t = t.back(1)
                if t.exists(ET):
                    b = t.slot(2)
                    if attention:
                        act.wait_ge(q_done, t.m + 1)
                        if t.reuses(2):
                            act.wait_ge(k_read, t.m - 1)
                        nc.scalar.activation(q[:, b, :], ps_q[:], ACT.Copy, scale=DH ** -0.5).then_inc(q_read, 1)
                    act.wait_ge(v_done, t.m + 1)
                    nc.scalar.activation(values[:, bass.ts(t.m, D)], ps_v[:], ACT.Copy).then_inc(v_read, 1)
            tiles(act, ET, 1, step)

        @f.block.tensor
        def _(pe):
            if not attention:
                pe.wait_ge(d_loaded, 48)
                pe.wait_ge(blocks_ready, 2)
                for w in range(2):
                    for m in range(KC):
                        for k in range(KC):
                            mm = pe.matmul(ps_d[:, w * KC * H + m * H:w * KC * H + (m + 1) * H],
                                           w_nat[:, k * D + m * P:k * D + (m + 1) * P], blocks[:, w, k, :],
                                           start=k == 0, stop=k == KC - 1)
                mm.then_inc(d_done, 1)
                pe.wait_ge(d_lo, 1)
            pe.wait_ge(W.lo_done, W.count)

            def step(t):
                if t.exists(ET):
                    b = t.slot(2)
                    for w, x, landed in (("o", xo, g_other), ("k", xk, g_key)):
                        pe.wait_ge(landed[b], 16 * t.turn(2) + 16)
                        if t.reuses(2):
                            pe.wait_ge(lo_done, 2 * (t.m - 1))
                        transpose_tile(pe, ps_t[w, b], x[:, b, :], s.ident).then_inc(turned, 1)
                t = t.back(1)
                if t.exists(ET):
                    b = t.slot(2)
                    hi = {w: part[w, "hi"][:, b, :] for w in "ok"}
                    lo = {w: part[w, "lo"][:, b, :] for w in "ok"}
                    pe.wait_ge(lo_done, 2 * t.m + 2)
                    if attention:
                        if t.reuses(1):
                            pe.wait_ge(q_read, t.m)
                        W.product(pe, ps_q[:], hi["k"], lo["k"], "q").then_inc(q_done, 1)
                        if t.reuses(1):
                            pe.wait_ge(k_read, t.m)
                        W.product(pe, ps_k[:], hi["o"], lo["o"], "k").then_inc(k_done, 1)
                    else:
                        if t.reuses(1):
                            pe.wait_ge(s_read, t.m)
                        n = 0
                        for w, x in ((0, "o"), (1, "k")):
                            for k in range(KC):
                                for xp, wp in ((hi, dhi), (hi, dlo), (lo, dhi)):
                                    mm = pe.matmul(ps_s[:, 0:H], xp[x][:, bass.ts(k, P)], wp[:, w, bass.ts(k, H)],
                                                   start=n == 0, stop=n == 6 * KC - 1)
                                    n += 1
                        mm.then_inc(s_done, 1)
                    if t.reuses(1):
                        pe.wait_ge(v_read, t.m)
                    W.product(pe, ps_v[:], hi["o"], lo["o"], "v").then_inc(v_done, 1)
            tiles(pe, ET, 1, step)


def softmax_weights(nc, s, order, name, scores, gat=False):
    EH = ET * H
    chunks = [(c, min(P, EH - c)) for c in range(0, EH, P)]
    NC = len(chunks)
    with phase(nc, name) as f:
        turned_sb = f.sb("turned_sb", [P, NC, P])
        by_head = f.sb("by_head", [H, SLOTS])
        brk = f.sb("brk", [H, SLOTS])
        fwd = f.sb("fwd", [H, SLOTS])
        back = f.sb("back", [H, SLOTS])
        back_sb = f.sb("back_sb", [P, NC, P])
        ps = [f.psum(f"ps{c}", [P, 512]) for c in range(NC)]
        ps2 = [f.psum(f"ps2{c}", [P, 512]) for c in range(NC)]
        masked, turned, copied, out1, in1 = (f.sem(n) for n in ("masked", "turned", "copied", "out1", "in1"))
        brk_in, back_done, out2, in2, turned2, chain, diff, loads = (f.sem(n) for n in (
            "brk_in", "back_done", "out2", "in2", "turned2", "chain", "diff", "loads"))
        if gat:
            emb = f.sb("emb", [P, NTYPE * H])
            gain = f.sb("gain", [P, EH])
            pick = f.sb("pick", [P, ET])
            term = f.sb("term", [P, EH])

        scratch_in, scratch_back = s.scratch

        @f.block.sync
        def _(sp):
            sp.dma_start(brk[:], order.breaks.rearrange("t p -> (t p)").partition_broadcast(H)).then_inc(brk_in, 16)
            if gat:
                sp.dma_start(emb[:], s.inputs["et_emb"].partition_broadcast(P)).then_inc(loads, 16)
            sp.wait_ge(copied, NC)
            for c, (lo, w) in enumerate(chunks):
                sp.dma_start(scratch_in[lo:lo + w, :], turned_sb[0:w, c, :]).then_inc(out1, 16)
            sp.wait_ge(out1, 16 * NC)
            sp.dma_start(by_head[:].rearrange("h (t s) -> h t s", s=P),
                         scratch_in.rearrange("(t h) s -> h t s", h=H)).then_inc(in1, 16)
            sp.wait_ge(back_done, 2)
            sp.dma_start(scratch_back.rearrange("(t h) s -> h t s", h=H),
                         back[:].rearrange("h (t s) -> h t s", s=P)).then_inc(out2, 16)
            sp.wait_ge(out2, 16)
            for c, (lo, w) in enumerate(chunks):
                sp.dma_start(back_sb[0:w, c, :], scratch_back[lo:lo + w, :]).then_inc(in2, 16)

        @f.block.vector
        def _(dve):
            n = [0]

            def link(ins):
                n[0] += 1
                ins.then_inc(chain, 1)
                dve.wait_ge(chain, n[0])

            sc = scores[:]
            if gat:
                link(nc.vector.tensor_scalar(term[:], sc, 0.2, None, ALU.mult))
                link(nc.vector.tensor_tensor(sc, sc, term[:], ALU.max))
                dve.wait_ge(loads, 16)
                link(nc.vector.memset(gain[:], 1.0))
                cube = [P, ET, H]
                v3 = lambda a: a.rearrange("p (t h) -> p t h", h=H)
                for k in range(NTYPE):
                    link(nc.vector.tensor_scalar(pick[:], order.type_col[:], float(k), None, ALU.is_equal))
                    link(nc.vector.tensor_tensor(v3(term[:]), pick[:].unsqueeze(2).to_broadcast(cube),
                                                 emb[:, bass.ts(k, H)].unsqueeze(1).to_broadcast(cube), ALU.mult))
                    link(nc.vector.tensor_tensor(gain[:], gain[:], term[:], ALU.add))
                link(nc.vector.tensor_tensor(sc, sc, gain[:], ALU.mult))
                link(nc.vector.tensor_tensor(v3(sc), v3(sc), order.weight_col[:].unsqueeze(2).to_broadcast(cube), ALU.mult))
            nc.vector.memset(scores[0:1, :], FAR).then_inc(masked, 1)
            for c, (lo, w) in enumerate(chunks):
                dve.wait_ge(turned, c + 1)
                nc.vector.tensor_copy(turned_sb[0:w, c, :], ps[c][0:w, 0:P]).then_inc(copied, 1)
            dve.wait_ge(in1, 16)
            dve.wait_ge(brk_in, 16)
            link(nc.vector.tensor_tensor_scan(fwd[:], brk[:], by_head[:], FAR, ALU.add, ALU.max))
            nc.vector.tensor_tensor_scan(back[:, 0:SLOTS - 1][:, ::-1], brk[:, 1:SLOTS][:, ::-1], fwd[:, 0:SLOTS - 1][:, ::-1],
                                         fwd[:, SLOTS - 1:SLOTS], ALU.add, ALU.max).then_inc(back_done, 1)
            nc.vector.tensor_copy(back[:, SLOTS - 1:SLOTS], fwd[:, SLOTS - 1:SLOTS]).then_inc(back_done, 1)
            dve.wait_ge(turned2, NC)
            for c, (lo, w) in enumerate(chunks):
                part = scores[:, lo:lo + w]
                if gat:
                    link(nc.vector.tensor_scalar(term[:, lo:lo + w], ps2[c][:, 0:w], 0.0, None, ALU.max))
                    top = term[:, lo:lo + w]
                else:
                    top = ps2[c][:, 0:w]
                nc.vector.tensor_tensor(part, part, top, ALU.subtract).then_inc(diff, 1)

        @f.block.tensor
        def _(pe):
            pe.wait_ge(masked, 1)
            for c, (lo, w) in enumerate(chunks):
                pe.transpose(ps[c][0:w, 0:P], scores[:, lo:lo + w], s.ident).then_inc(turned, 1)
            pe.wait_ge(in2, 16 * NC)
            for c, (lo, w) in enumerate(chunks):
                pe.transpose(ps2[c][:, 0:w], back_sb[0:w, c, :], s.ident[0:w, 0:w]).then_inc(turned2, 1)

        @f.block.scalar
        def _(act):
            act.wait_ge(diff, NC)
            nc.scalar.activation(scores[:], scores[:], ACT.Exp)



def node_sage(nc, s, order):
    with phase(nc, "sage") as f:
        x, u, g = f.sb("x", [P, 4, D]), f.sb("u", [P, 4, D]), f.sb("g", [P, 4, D])
        t_sum, r, y, z = (f.sb(n, [P, 2, D]) for n in ("t_sum", "r", "y", "z"))
        stats, mv, dev, rstd = f.sb("stats", [P, 2, 6]), f.sb("mv", [P, 2, 2]), f.sb("dev", [P, 2, 1]), f.sb("rstd", [P, 2, 1])
        dev_done = f.sem("dev_done")
        stage = f.sb("stage", [P, 4], I32)
        loaded = [f.sem(f"loaded{b}") for b in range(4)]
        gathered = [f.sem(f"gathered{b}") for b in range(4)]
        stored = [f.sem(f"stored{b}") for b in range(2)]
        staged, summed, rect, steps_s = f.sem("staged"), f.sem("summed"), f.sem("rect"), f.sem("steps")

        @f.block.sync
        def _(sp):
            def step(t):
                if t.exists(NT):
                    r4 = t.slot(4)
                    if t.reuses(4):
                        sp.wait_ge(steps_s, 5 * (t.m - 3))
                    sp.dma_start(x[:, r4, :], rows(s.inputs["x"], t.m)).then_inc(loaded[r4], 16)
                    sp.dma_start(u[:, r4, :], rows(s.root, t.m)).then_inc(loaded[r4], 16)
                t = t.back(3)
                if t.exists(NT):
                    sp.wait_ge(steps_s, 5 * t.m + 5)
                    sp.dma_start(rows(s.x1, t.m), z[:, t.slot(2), :]).then_inc(stored[t.slot(2)], 16)
            tiles(sp, NT, 3, step)
            for b in range(2):
                sp.wait_ge(stored[b], 16 * (NT // 2))

        @f.block.gpsimd
        def _(pool):
            def step(t):
                r4 = t.slot(4)
                if t.reuses(4):
                    pool.wait_ge(summed, t.m - 3)
                    pool.wait_ge(gathered[r4], 16 * t.turn(4))
                gather(nc, pool, f.passed_pool, (staged, 1, 1), t, order.place, stage[:, r4:r4 + 1], s.edge_out, g[:, r4, :], gathered[r4])
            tiles(pool, NT, 0, step)

        @f.block.vector
        def _(dve):
            steps = Steps(dve, steps_s, 5)

            def step(t):
                now, before = t, t.back(1)
                if before.exists(NT):
                    b, r4 = before.slot(2), before.slot(4)
                    st = steps.tile(before.m)
                    dve.wait_ge(rect, before.m + 1)
                    st(nc.vector.scalar_tensor_tensor(y[:, b, :], x[:, r4, :], 2.0, r[:, b, :], ALU.mult, ALU.add))
                    norm_stats(nc, st, f.passed_dve, stats[:, b, :], mv[:, b, :], y[:, b, :])
                if now.exists(NT):
                    b, r4 = now.slot(2), now.slot(4)
                    dve.wait_ge(loaded[r4], 32 * now.turn(4) + 32)
                    dve.wait_ge(gathered[r4], 16 * now.turn(4) + 16)
                    if now.reuses(2):
                        dve.wait_ge(rect, now.m - 1)
                    nc.vector.tensor_tensor(t_sum[:, b, :], u[:, r4, :], g[:, r4, :], ALU.add).then_inc(summed, 1)
                if before.exists(NT):
                    b = before.slot(2)
                    dve.wait_ge(dev_done, before.m + 1)
                    st(nc.vector.reciprocal(rstd[:, b, :], dev[:, b, :]))
                    if before.reuses(2):
                        dve.wait_ge(stored[b], 16 * before.turn(2))
                    st.last(nc.vector.tensor_scalar(z[:, b, :], y[:, b, :], mv[:, b, 0:1], rstd[:, b, :], ALU.subtract, ALU.mult))
            tiles(dve, NT, 1, step)

        @f.block.scalar
        def _(act):
            nc.scalar.preload_act_table(ACT.Sqrt)

            def step(t):
                now, before = t, t.back(1)
                if before.exists(NT):
                    b = before.slot(2)
                    act.wait_ge(steps_s, 5 * before.m + 3)
                    deviation(nc, s, dev[:, b, :], mv[:, b, :]).then_inc(dev_done, 1)
                if now.exists(NT):
                    b = now.slot(2)
                    act.wait_ge(summed, now.m + 1)
                    if now.reuses(2):
                        act.wait_ge(steps_s, 5 * (now.m - 1))
                    nc.scalar.activation(r[:, b, :], t_sum[:, b, :], ACT.Relu).then_inc(rect, 1)
            tiles(act, NT, 1, step)


def add_tiles(pe, s, out, tiles_in):
    for j, t in enumerate(tiles_in):
        mm = pe.matmul(out, s.ident, t, start=j == 0, stop=j == len(tiles_in) - 1)
    return mm


class Norm:

    def __init__(self, nc, f, s, name, ring):
        self.nc, self.f, self.s, self.ring = nc, f, s, ring
        self.st, self.mv = f.sb(f"{name}_st", [P, ring, 6]), f.sb(f"{name}_mv", [P, ring, 2])
        self.dev, self.rs = f.sb(f"{name}_dev", [P, ring, 1]), f.sb(f"{name}_rs", [P, ring, 2])
        self.stats_done, self.dev_done, self.scale_done = f.sem(f"{name}_stats"), f.sem(f"{name}_dev"), f.sem(f"{name}_scale")

    def stats(self, dve, t, x):
        r = t.slot(self.ring)
        steps = Steps(dve, self.stats_done, 2).tile(t.m)
        norm_stats(self.nc, steps, self.f.passed_dve, self.st[:, r, :], self.mv[:, r, :], x)

    def root(self, act, t):
        r = t.slot(self.ring)
        act.wait_ge(self.stats_done, 2 * t.m + 2)
        deviation(self.nc, self.s, self.dev[:, r, :], self.mv[:, r, :]).then_inc(self.dev_done, 1)

    def scale(self, dve, t):
        r = t.slot(self.ring)
        steps = Steps(dve, self.scale_done, 2).tile(t.m)
        dve.wait_ge(self.dev_done, t.m + 1)
        norm_scale(self.nc, steps, self.mv[:, r, :], self.dev[:, r, :], self.rs[:, r, :])

    def apply(self, act, t, out, x):
        r = t.slot(self.ring)
        act.wait_ge(self.scale_done, 2 * t.m + 2)
        return self.nc.scalar.activation(out, x, ACT.Identity, bias=self.rs[:, r, 1:2], scale=self.rs[:, r, 0:1])


def node_ffn(nc, s, order):
    with phase(nc, "ffn") as f:
        U, F1 = 8, DFF + 1
        x, g, y, z1 = (f.sb(n, [P, r, D]) for n, r in (("x", 8), ("g", 4), ("y", 2), ("z1", 2)))
        zt = f.sb("zt", [P, 4, D])
        hid = f.sb("hid", [F1, 4, P])
        z2, gained, xb, y3, z3 = (f.sb(n, [P, r, D]) for n, r in (("z2", 2), ("gained", 2), ("xb", 4), ("y3", 2), ("z3", 2)))
        stage = f.sb("stage", [P, 4], I32)
        g2, b2n = f.sb("g2", [P, D]), f.sb("b2n", [P, D])
        gcol, bcol, b1, bias1 = f.sb("gcol", [P, KC]), f.sb("bcol", [P, KC]), f.sb("b1", [DFF, 1]), f.sb("bias1", [DFF, 1])
        w1, w1s = f.sb("w1", [P, KC * DFF]), f.sb("w1s", [P, KC * DFF])
        w2, shifts = f.sb("w2", [F1, D]), f.sb("shifts", [F1, 2, D])
        diag = f.sb("diag", [P, KC, P])
        n1, n2, n3 = Norm(nc, f, s, "n1", 2), Norm(nc, f, s, "n2", 2), Norm(nc, f, s, "n3", 2)
        ps_t = [f.psum(f"t{b}", [P, D]) for b in range(2)]
        ps_h = [f.psum(f"h{b}", [P, D]) for b in range(2)]
        ps_f = [f.psum(f"f{b}", [P, D]) for b in range(4)]
        params, set_up, bias_made, bias_ready = (f.sem(n) for n in ("params", "set_up", "bias_made", "bias_ready"))
        loaded = [f.sem(f"loaded{b}") for b in range(8)]
        gathered = [f.sem(f"gathered{b}") for b in range(4)]
        stored = [f.sem(f"stored{b}") for b in range(2)]
        staged, y_done, z1_done, turned, zt_done, h_done, relu_done, f_done = (f.sem(n) for n in (
            "staged", "y_done", "z1_done", "turned", "zt_done", "h_done", "relu_done", "f_done"))
        z2_done, gain_done, xb_done, y3_done, z3_done = (f.sem(n) for n in ("z2_done", "gain_done", "xb_done", "y3_done", "z3_done"))
        SETUP = 3 + 2 * KC

        @f.block.sync
        def _(sp):
            for ap, src in ((gcol[:], "ln1_g_col"), (bcol[:], "ln1_b_col"), (b1[:], "b1_col"), (w2[0:DFF, :], "w2")):
                sp.dma_start(ap, s.inputs[src]).then_inc(params, 16)
            sp.dma_start(w1[:].rearrange("p (k n) -> p k n", n=DFF), s.inputs["w1"].rearrange("(k p) n -> p k n", p=P)).then_inc(params, 16)
            for j, src in enumerate(("ln1_b", "b2")):
                sp.dma_start(shifts[DFF:F1, j, :], s.inputs[src].partition_broadcast(1)).then_inc(params, 16)
            for ap, src in ((g2, "ln2_g"), (b2n, "ln2_b")):
                sp.dma_start(ap[:], s.inputs[src].partition_broadcast(P)).then_inc(params, 16)

            def step(t):
                if t.exists(NT):
                    r = t.slot(8)
                    if t.reuses(8):
                        sp.wait_ge(xb_done, t.m - 7)
                    sp.dma_start(x[:, r, :], rows(s.x1, t.m)).then_inc(loaded[r], 16)
                t = t.back(9)
                if t.exists(NT):
                    sp.wait_ge(z3_done, t.m + 1)
                    sp.dma_start(rows(s.x2, t.m), z3[:, t.slot(2), :]).then_inc(stored[t.slot(2)], 16)
            tiles(sp, NT, 9, step, U, 2)
            for b in range(2):
                sp.wait_ge(stored[b], 16 * (NT // 2))

        @f.block.gpsimd
        def _(pool):
            pool.wait_ge(params, 144)

            def step(t):
                t5, t7 = t.back(5), t.back(7)
                if t.exists(NT):
                    r = t.slot(4)
                    if t.reuses(4):
                        pool.wait_ge(y_done, t.m - 3)
                        pool.wait_ge(gathered[r], 16 * t.turn(4))
                    gather(nc, pool, f.passed_pool, (staged, 1, 1), t, order.place, stage[:, r:r + 1], s.edge_out, g[:, r, :], gathered[r])
                if t7.exists(NT):
                    b = t7.slot(2)
                    pool.wait_ge(z2_done, t7.m + 1)
                    if t7.reuses(2):
                        pool.wait_ge(y3_done, t7.m - 1)
                    nc.gpsimd.tensor_tensor(gained[:, b, :], z2[:, b, :], g2[:], ALU.mult).then_inc(gain_done, 1)
                if t5.exists(NT):
                    pool.wait_ge(loaded[t5.slot(8)], 16 * t5.turn(8) + 16)
                    if t5.reuses(4):
                        pool.wait_ge(y3_done, t5.m - 3)
                    nc.gpsimd.tensor_tensor(xb[:, t5.slot(4), :], x[:, t5.slot(8), :], b2n[:], ALU.add).then_inc(xb_done, 1)
            tiles(pool, NT, 7, step, U)

        @f.block.vector
        def _(dve):
            dve.wait_ge(params, 144)
            nc.vector.tensor_tensor(w2[DFF:F1, :], shifts[DFF:F1, 0, :], shifts[DFF:F1, 1, :], ALU.add).then_inc(set_up, 1)
            nc.vector.memset(hid[DFF:F1, :, :], 1.0).then_inc(set_up, 1)
            for k in range(KC):
                nc.vector.tensor_scalar(diag[:, k, :], s.ident, gcol[:, k:k + 1], None, ALU.mult).then_inc(set_up, 1)
                nc.vector.tensor_scalar(w1s[:, bass.ts(k, DFF)], w1[:, bass.ts(k, DFF)], gcol[:, k:k + 1], None, ALU.mult).then_inc(set_up, 1)
            dve.wait_ge(bias_made, 1)
            nc.vector.tensor_tensor(bias1[:], b1[:], ps_h[0][0:DFF, 0:1], ALU.add).then_inc(set_up, 1)

            def step(t):
                t4, t5 = t.back(4), t.back(5)
                if t4.exists(NT):
                    dve.wait_ge(f_done, t4.m + 1)
                    n2.stats(dve, t4, ps_f[t4.slot(4)][:])
                if t.exists(NT):
                    b = t.slot(2)
                    dve.wait_ge(loaded[t.slot(8)], 16 * t.turn(8) + 16)
                    dve.wait_ge(gathered[t.slot(4)], 16 * t.turn(4) + 16)
                    if t.reuses(2):
                        dve.wait_ge(z1_done, t.m - 1)
                    nc.vector.tensor_tensor(y[:, b, :], x[:, t.slot(8), :], g[:, t.slot(4), :], ALU.add).then_inc(y_done, 1)
                    dve.wait_ge(y_done, t.m + 1)
                    n1.stats(dve, t, y[:, b, :])
                if t5.exists(NT):
                    b = t5.slot(2)
                    dve.wait_ge(gain_done, t5.m + 1)
                    dve.wait_ge(xb_done, t5.m + 1)
                    if t5.reuses(2):
                        dve.wait_ge(z3_done, t5.m - 1)
                    nc.vector.tensor_tensor(y3[:, b, :], gained[:, b, :], xb[:, t5.slot(4), :], ALU.add).then_inc(y3_done, 1)
                    dve.wait_ge(y3_done, t5.m + 1)
                    n3.stats(dve, t5, y3[:, b, :])
                if t4.exists(NT):
                    n2.scale(dve, t4)
                if t.exists(NT):
                    n1.scale(dve, t)
                if t5.exists(NT):
                    n3.scale(dve, t5)
            tiles(dve, NT, 5, step, U)

        @f.block.scalar
        def _(act):
            nc.scalar.preload_act_table(ACT.Sqrt)
            act.wait_ge(set_up, SETUP)

            def step(t):
                t1, t2, t4, t5 = t.back(1), t.back(2), t.back(4), t.back(5)
                if t4.exists(NT):
                    n2.root(act, t4)
                if t1.exists(NT):
                    act.wait_ge(turned, t1.m + 1)
                    if t1.reuses(4):
                        act.wait_ge(f_done, t1.m - 3)
                    nc.scalar.activation(zt[:, t1.slot(4), :], ps_t[t1.slot(2)][:], ACT.Copy).then_inc(zt_done, 1)
                if t2.exists(NT):
                    act.wait_ge(h_done, t2.m + 1)
                    if t2.reuses(4):
                        act.wait_ge(f_done, t2.m - 3)
                    nc.scalar.activation(hid[0:DFF, t2.slot(4), :], ps_h[t2.slot(2)][0:DFF, 0:P], ACT.Relu, bias=bias1[:]).then_inc(relu_done, 1)
                if t.exists(NT):
                    n1.root(act, t)
                if t5.exists(NT):
                    n3.root(act, t5)
                if t4.exists(NT):
                    if t4.reuses(2):
                        act.wait_ge(gain_done, t4.m - 1)
                    n2.apply(act, t4, z2[:, t4.slot(2), :], ps_f[t4.slot(4)][:]).then_inc(z2_done, 1)
                if t.exists(NT):
                    b = t.slot(2)
                    if t.reuses(2):
                        act.wait_ge(turned, t.m - 1)
                    n1.apply(act, t, z1[:, b, :], y[:, b, :]).then_inc(z1_done, 1)
                if t5.exists(NT):
                    b = t5.slot(2)
                    if t5.reuses(2):
                        act.wait_ge(stored[b], 16 * t5.turn(2))
                    n3.apply(act, t5, z3[:, b, :], y3[:, b, :]).then_inc(z3_done, 1)
            tiles(act, NT, 5, step, U)

        @f.block.tensor
        def _(pe):
            pe.wait_ge(params, 144)
            for k in range(KC):
                mm = pe.matmul(ps_h[0][0:DFF, 0:1], w1[:, bass.ts(k, DFF)], bcol[:, k:k + 1], start=k == 0, stop=k == KC - 1)
            mm.then_inc(bias_made, 1)
            pe.wait_ge(set_up, SETUP)

            def step(t):
                t1, t2, t3 = t.back(1), t.back(2), t.back(3)
                if t1.exists(NT):
                    b = t1.slot(2)
                    pe.wait_ge(z1_done, t1.m + 1)
                    if t1.reuses(2):
                        pe.wait_ge(zt_done, t1.m - 1)
                    transpose_tile(pe, ps_t[b], z1[:, b, :], s.ident).then_inc(turned, 1)
                if t2.exists(NT):
                    b = t2.slot(2)
                    pe.wait_ge(zt_done, t2.m + 1)
                    if t2.reuses(2):
                        pe.wait_ge(relu_done, t2.m - 1)
                    for k in range(KC):
                        mm = pe.matmul(ps_h[b][0:DFF, 0:P], w1s[:, bass.ts(k, DFF)], zt[:, t2.slot(4), bass.ts(k, P)],
                                       start=k == 0, stop=k == KC - 1)
                    mm.then_inc(h_done, 1)
                if t3.exists(NT):
                    r = t3.slot(4)
                    pe.wait_ge(relu_done, t3.m + 1)
                    if t3.reuses(4):
                        pe.wait_ge(z2_done, t3.m - 3)
                    pe.matmul(ps_f[r][:], hid[:, r, :], w2[:], start=True, stop=False, skip_group_check=True)
                    for k in range(KC):
                        mm = pe.matmul(ps_f[r][:, bass.ts(k, P)], zt[:, r, bass.ts(k, P)], diag[:, k, :],
                                       start=False, stop=k == KC - 1, skip_group_check=True)
                    mm.then_inc(f_done, 1)
            tiles(pe, NT, 3, step, U)


def node_residual(nc, s, order, name, x_in, x_out, affine=None):
    with phase(nc, name) as f:
        U = 8
        x, g, z = f.sb("x", [P, 8, D]), f.sb("g", [P, 4, D]), f.sb("z", [P, 2, D])
        stage = f.sb("stage", [P, 4], I32)
        n1 = Norm(nc, f, s, "n1", 2)
        ps_y = [f.psum(f"y{b}", [P, D]) for b in range(4)]
        loaded = [f.sem(f"loaded{b}") for b in range(8)]
        gathered = [f.sem(f"gathered{b}") for b in range(4)]
        stored = [f.sem(f"stored{b}") for b in range(2)]
        staged, y_done, z_done = f.sem("staged"), f.sem("y_done"), f.sem("z_done")
        if affine:
            z1, gained, y2, xb = (f.sb(n, [P, r, D]) for n, r in (("z1", 4), ("gained", 2), ("y2", 2), ("xb", 4)))
            gain, shift = f.sb("gain", [P, D]), f.sb("shift", [P, D])
            n2 = Norm(nc, f, s, "n2", 2)
            params, z1_done, gain_done, xb_done, y2_done = (f.sem(n) for n in ("params", "z1_done", "gain_done", "xb_done", "y2_done"))
        L = 2 if affine else 0
        SL = 6 if affine else 4

        @f.block.sync
        def _(sp):
            if affine:
                for ap, src in zip((gain, shift), affine):
                    sp.dma_start(ap[:], src.partition_broadcast(P)).then_inc(params, 16)

            def step(t):
                if t.exists(NT):
                    r = t.slot(8)
                    if t.reuses(8):
                        sp.wait_ge(y_done, t.m - 7)
                        if affine:
                            sp.wait_ge(xb_done, t.m - 7)
                    sp.dma_start(x[:, r, :], rows(x_in, t.m)).then_inc(loaded[r], 16)
                t = t.back(SL)
                if t.exists(NT):
                    sp.wait_ge(z_done, t.m + 1)
                    sp.dma_start(rows(x_out, t.m), z[:, t.slot(2), :]).then_inc(stored[t.slot(2)], 16)
            tiles(sp, NT, SL, step, U)
            for b in range(2):
                sp.wait_ge(stored[b], 16 * (NT // 2))

        @f.block.gpsimd
        def _(pool):
            if affine:
                pool.wait_ge(params, 32)

            def step(t):
                if t.exists(NT):
                    r = t.slot(4)
                    if t.reuses(4):
                        pool.wait_ge(y_done, t.m - 3)
                        pool.wait_ge(gathered[r], 16 * t.turn(4))
                    gather(nc, pool, f.passed_pool, (staged, 1, 1), t, order.place, stage[:, r:r + 1], s.edge_out, g[:, r, :], gathered[r])
                t = t.back(2)
                if affine and t.exists(NT):
                    pool.wait_ge(loaded[t.slot(8)], 16 * t.turn(8) + 16)
                    if t.reuses(4):
                        pool.wait_ge(y2_done, t.m - 3)
                    nc.gpsimd.tensor_tensor(xb[:, t.slot(4), :], x[:, t.slot(8), :], shift[:], ALU.add).then_inc(xb_done, 1)
            tiles(pool, NT, L, step, U)

        @f.block.tensor
        def _(pe):
            def step(t):
                r = t.slot(4)
                pe.wait_ge(loaded[t.slot(8)], 16 * t.turn(8) + 16)
                pe.wait_ge(gathered[r], 16 * t.turn(4) + 16)
                if t.reuses(4):
                    pe.wait_ge(z1_done if affine else z_done, t.m - 3)
                add_tiles(pe, s, ps_y[r][:], (x[:, t.slot(8), :], g[:, r, :])).then_inc(y_done, 1)
            tiles(pe, NT, 0, step, U)

        @f.block.vector
        def _(dve):
            if affine:
                dve.wait_ge(params, 32)

            def step(t):
                t1, t2 = t.back(1), t.back(2)
                if t.exists(NT):
                    dve.wait_ge(y_done, t.m + 1)
                    n1.stats(dve, t, ps_y[t.slot(4)][:])
                if affine and t2.exists(NT):
                    b = t2.slot(2)
                    dve.wait_ge(z1_done, t2.m + 1)
                    nc.vector.tensor_tensor(gained[:, b, :], z1[:, t2.slot(4), :], gain[:], ALU.mult).then_inc(gain_done, 1)
                    dve.wait_ge(gain_done, t2.m + 1)
                    dve.wait_ge(xb_done, t2.m + 1)
                    if t2.reuses(2):
                        dve.wait_ge(z_done, t2.m - 1)
                    nc.vector.tensor_tensor(y2[:, b, :], gained[:, b, :], xb[:, t2.slot(4), :], ALU.add).then_inc(y2_done, 1)
                    dve.wait_ge(y2_done, t2.m + 1)
                    n2.stats(dve, t2, y2[:, b, :])
                if affine:
                    if t.exists(NT):
                        n1.scale(dve, t)
                    if t2.exists(NT):
                        n2.scale(dve, t2)
                elif t1.exists(NT):
                    n1.scale(dve, t1)
            tiles(dve, NT, 2 if affine else 1, step, U)

        @f.block.scalar
        def _(act):
            nc.scalar.preload_act_table(ACT.Sqrt)

            def step(t):
                t1, t2 = t.back(1), t.back(2)
                if t.exists(NT):
                    n1.root(act, t)
                if not affine:
                    if t1.exists(NT):
                        b = t1.slot(2)
                        if t1.reuses(2):
                            act.wait_ge(stored[b], 16 * t1.turn(2))
                        n1.apply(act, t1, z[:, b, :], ps_y[t1.slot(4)][:]).then_inc(z_done, 1)
                    return
                if t2.exists(NT):
                    n2.root(act, t2)
                if t.exists(NT):
                    if t.reuses(4):
                        act.wait_ge(gain_done, t.m - 3)
                    n1.apply(act, t, z1[:, t.slot(4), :], ps_y[t.slot(4)][:]).then_inc(z1_done, 1)
                if t2.exists(NT):
                    b = t2.slot(2)
                    if t2.reuses(2):
                        act.wait_ge(stored[b], 16 * t2.turn(2))
                    n2.apply(act, t2, z[:, b, :], y2[:, b, :]).then_inc(z_done, 1)
            tiles(act, NT, 2 if affine else 1, step, U)



def gnn_program(nc, a, out):
    with ExitStack() as ctx:
        def sb(n, shape, dt=F32):
            return ctx.enter_context(nc.sbuf_tensor(n, shape, dt))

        def dram(n, shape, dt=F32):
            return nc.dram_tensor(n, shape, dt, kind="Internal").ap()

        s = Names()
        s.inputs = a
        s.packed = sb("packed", [P, CW])
        s.root, s.x1, s.x2, s.x3 = (dram(n, [NP, D]) for n in ("root_d", "x1_d", "x2_d", "x3_d"))
        s.edge_out = dram("edge_out_d", [SLOTS + P, D])
        s.scratch = [dram(f"scratch{i}_d", [ET * H, P]) for i in range(2)]
        s.iota, s.ident, s.earlier, s.above, s.ones, s.zrow = (s.packed[:, j * P:(j + 1) * P] for j in range(len(CONSTS)))
        c = len(CONSTS) * P
        s.heads = s.packed[:, c:c + KC * H].rearrange("p (k h) -> p k h", h=H)
        s.part = s.packed[:, c + KC * H:c + KC * H + 1]
        s.eps = s.packed[:, c + KC * H + 1:c + KC * H + 2]

        def order(key):
            o = Names()
            o.key = key
            o.table = dram(f"table{key}_d", [SLOTS, 4])
            o.key_out = dram(f"key_out{key}_d", [SLOTS])
            o.key_in = dram(f"key_in{key}_d", [ET, P])
            o.breaks = dram(f"breaks{key}_d", [ET, P])
            o.key_in_col = sb(f"key_in_col{key}", [P, ET])
            o.other_idx, o.key_idx = sb(f"other_idx{key}", [P, ET], I32), sb(f"key_idx{key}", [P, ET], I32)
            o.type_col, o.weight_col = sb(f"type_col{key}", [P, ET]), sb(f"weight_col{key}", [P, ET])
            o.place = sb(f"place{key}", [P, NT], I32)
            return o

        by_dst, by_src = order(DST), order(SRC)
        load_constants(nc, s)
        sort_edges(nc, s, by_dst)
        sort_edges(nc, s, by_src)

        dense_root(nc, s)
        aggregate(nc, s, by_dst, "agg0", source=s.inputs["x"], matrix=s.inputs["wl_t"])
        node_sage(nc, s, by_dst)

        with nc.sbuf_tensor("values", [P, ET * D], F32) as values, nc.sbuf_tensor("scores", [P, ET * H], F32) as scores:
            edge_products(nc, s, by_dst, "qkv1", s.x1, {"k": (s.inputs["wk"], D), "v": (s.inputs["wv"], D)}, {"q": (s.inputs["wq"], D)}, values, scores)
            softmax_weights(nc, s, by_dst, "soft1", scores)
            aggregate(nc, s, by_dst, "agg1", values=values, weights=scores, matrix=s.inputs["wo"])
        node_ffn(nc, s, by_dst)

        with nc.sbuf_tensor("values2", [P, ET * D], F32) as values, nc.sbuf_tensor("scores2", [P, ET * H], F32) as scores:
            edge_products(nc, s, by_dst, "gat2", s.x2, {"v": (s.inputs["w_gat_t"], D)}, {}, values, scores,
                          dots=("w_gat", "a_src_col", "a_dst_col"))
            softmax_weights(nc, s, by_dst, "soft2", scores, gat=True)
            aggregate(nc, s, by_dst, "agg2", values=values, weights=scores, small=1e-10)
        node_residual(nc, s, by_dst, "res2", s.x2, s.x3, affine=(s.inputs["gat_g"], s.inputs["gat_b"]))

        with nc.sbuf_tensor("values3", [P, ET * D], F32) as values, nc.sbuf_tensor("scores3", [P, ET * H], F32) as scores:
            edge_products(nc, s, by_src, "qkv3", s.x3, {"k": (s.inputs["w3"][:, D:2 * D], D), "v": (s.inputs["w3"][:, 2 * D:3 * D], D)},
                          {"q": (s.inputs["w3"][:, 0:D], D)}, values, scores)
            softmax_weights(nc, s, by_src, "soft3", scores)
            aggregate(nc, s, by_src, "agg3", values=values, weights=scores)
        node_residual(nc, s, by_src, "res3", s.x3, out)


def kernel(**inputs):
    import concourse.bacc as bacc
    from concourse.bass_utils import run_bass_kernel_spmd

    v = {k: np.asarray(a) for k, a in inputs.items()}
    flip = lambda m: np.ascontiguousarray(m.T)
    col = lambda m: np.ascontiguousarray(m.reshape(-1, P).T)
    edge_col = lambda m: np.ascontiguousarray(m.reshape(ET, EC).T)
    packed, table = host_constants()
    x = np.zeros((NP, D), v["x"].dtype)
    x[:N] = v["x"]
    arrays = {
        "x": x, "consts_dram": packed, "table_default": table,
        "src_flat": v["src"], "dst_flat": v["dst"], "src_col": edge_col(v["src"]), "dst_col": edge_col(v["dst"]),
        "type_col": edge_col(v["edge_type_8"]), "weight_col": edge_col(v["edge_weight"]),
        "ln0_g_col": col(v["L0_gnn_ln_gamma"]), "ln0_b_col": col(v["L0_gnn_ln_beta"]),
        "wl_t": flip(v["L0_gnn_w_l"]), "wr_t": flip(v["L0_gnn_w_r"]), "b_l": v["L0_gnn_b_l"],
        "wq": v["L1_gnn_Wq"], "wk": v["L1_gnn_Wk"], "wv": v["L1_gnn_Wv"], "wo": v["L1_gnn_Wo"],
        "ln1_g": v["L1_gnn_ln1_g"], "ln1_b": v["L1_gnn_ln1_b"], "ln2_g": v["L1_gnn_ln2_g"], "ln2_b": v["L1_gnn_ln2_b"],
        "ln1_g_col": col(v["L1_gnn_ln1_g"]), "ln1_b_col": col(v["L1_gnn_ln1_b"]),
        "w1": v["L1_gnn_W1"], "b1_col": v["L1_gnn_b1"].reshape(DFF, 1), "w2": v["L1_gnn_W2"], "b2": v["L1_gnn_b2"],
        "w_gat": v["L2_gnn_W"], "w_gat_t": flip(v["L2_gnn_W"]),
        "a_src_col": col(v["L2_gnn_a_src"].reshape(-1)), "a_dst_col": col(v["L2_gnn_a_dst"].reshape(-1)),
        "et_emb": v["L2_gnn_et_emb"].reshape(-1), "gat_g": v["L2_gnn_ln_gamma"], "gat_b": v["L2_gnn_ln_beta"],
        "w3": v["L3_gnn_W"],
    }
    arrays = {k: np.ascontiguousarray(m) for k, m in arrays.items()}
    nc = bacc.Bacc("TRN2", target_bir_lowering=False, num_devices=1)
    aps = {k: nc.dram_tensor(f"in_{k}", m.shape, mybir.dt.from_np(m.dtype), kind="ExternalInput").ap() for k, m in arrays.items()}
    out = nc.dram_tensor("out", [NP, D], F32, kind="ExternalOutput").ap()
    gnn_program(nc, aps, out)
    r = run_bass_kernel_spmd(nc, [{f"in_{k}": m for k, m in arrays.items()}], core_ids=[0])
    return r.results[0]["out"][:N]
```
